# Optimizing a Trainium2 kernel written in Bass

```python
import numpy as np
import jax
import jax.numpy as jnp

def _softmax(x, axis=-1):
    return jax.nn.softmax(x, axis=axis)

def _gelu(x):
    return jax.nn.gelu(x, approximate=True)

def _silu(x):
    return jax.nn.silu(x)

def _sigmoid(x):
    return jax.nn.sigmoid(x)

def _layernorm(x, axis=-1, eps=1e-05):
    m = jnp.mean(x, axis=axis, keepdims=True)
    v = jnp.var(x, axis=axis, keepdims=True)
    return (x - m) / jnp.sqrt(v + eps)

def _scatter_add(tgt, idx, src, axis=0):
    return tgt.at[idx].add(src)

def _segment_sum(src, seg, n):
    return jax.ops.segment_sum(src, seg, n)
kernel_name = 'mk_flamingo_gated_d1_seqx_r2_d42bd2'

def setup_inputs(seed: int=0):
    np.random.seed(seed)
    _w = jnp.asarray

    def _rec_inputs():
        import jax
        import jax.numpy as jnp
        _rk = jax.random.key(seed)
        x = 0.001912 + 0.9994 * jax.random.normal(jax.random.fold_in(_rk, 1), (8, 224, 512), jnp.float32)
        _lenS = 224 - jax.random.randint(jax.random.fold_in(_rk, 7), (8,), 0, max(1, 224 // 4) + 1, jnp.int32)
        _lenS2 = 750 - jax.random.randint(jax.random.fold_in(_rk, 8), (8,), 0, max(1, 750 // 4) + 1, jnp.int32)
        _ctx_1024P = jax.random.normal(jax.random.fold_in(_rk, 11), (8, 16, 512), jnp.float32)
        _ctx_1024c = jax.random.dirichlet(jax.random.fold_in(_rk, 511), 0.3 * jnp.ones((16,), jnp.float32), (8, 750))
        _ctx_1024t = jnp.einsum('bsk,bkd->bsd', _ctx_1024c, _ctx_1024P)
        _ctx_1024t = _ctx_1024t * jax.lax.rsqrt(jnp.mean(jnp.square(_ctx_1024t)) + 1e-12) * 0.953939
        ctx_1024 = -0.000125008 + 0.999885 * (_ctx_1024t + 0.3 * jax.random.normal(jax.random.fold_in(_rk, 611), (8, 750, 512), jnp.float32))
        _g = jax.random.normal(jax.random.fold_in(_rk, 9001), (2, 1), jnp.float32)
        _g = jnp.sign(_g) * jnp.maximum(jnp.abs(_g), 1.0) + (_g == 0) * 1.0
        g_xattn = _g[0]
        g_ffn = _g[1]
        return (x, ctx_1024, g_xattn, g_ffn)
    x, ctx_1024, g_xattn, g_ffn = _rec_inputs()

    def _L0_xattn_setup():
        import jax, jax.numpy as jnp
        import numpy as np
        D_MODEL = 512
        D_HEAD = 64
        NHEADS = 8
        IN_DIM = D_HEAD * NHEADS
        EPS = 1e-05

        def layernorm(x, g, b):
            mu = jnp.mean(x, axis=-1, keepdims=True)
            var = jnp.var(x, axis=-1, keepdims=True)
            return (x - mu) * jax.lax.rsqrt(var + EPS) * g + b
        key = jax.random.key(seed)
        ks = jax.random.split(key, 8)
        B, M, L = (4, 4096, 64)
        x = jax.random.normal(ks[0], (B, M, D_MODEL), dtype=jnp.float32)
        latents = jax.random.normal(ks[1], (B, L, D_MODEL), dtype=jnp.float32)
        s = 1.0 / np.sqrt(D_MODEL)
        Wq = jax.random.normal(ks[2], (D_MODEL, IN_DIM), dtype=jnp.float32) * s
        Wkv = jax.random.normal(ks[3], (D_MODEL, 2 * IN_DIM), dtype=jnp.float32) * s
        Wout = jax.random.normal(ks[4], (IN_DIM, D_MODEL), dtype=jnp.float32) * (1.0 / np.sqrt(IN_DIM))
        gm = jnp.ones((D_MODEL,), jnp.float32)
        bm = jnp.zeros((D_MODEL,), jnp.float32)
        gl = jnp.ones((D_MODEL,), jnp.float32)
        bl = jnp.zeros((D_MODEL,), jnp.float32)
        return {'x': x, 'latents': latents, 'Wq': Wq, 'Wkv': Wkv, 'Wout': Wout, 'gm': gm, 'bm': bm, 'gl': gl, 'bl': bl}
    _L0_xattn_all = _L0_xattn_setup()
    _L0_xattn_in = {k: v for k, v in _L0_xattn_all.items() if k in ('Wq', 'Wkv', 'Wout', 'gm', 'bm', 'gl', 'bl')}
    del _L0_xattn_all

    def _L0_ffn_setup():
        import jax, jax.numpy as jnp
        import numpy as np
        import math
        BETA = 0.9
        THRESHOLD = 1.0
        NUM_STEPS = 5
        ALPHA = 2.0

        @jax.custom_vjp
        def spike_fn(u):
            return (u > 0).astype(u.dtype)

        def _spike_fwd(u):
            return (spike_fn(u), u)

        def _spike_bwd(u, g):
            s = jnp.pi / 2.0 * ALPHA * u
            return (g * (ALPHA / 2.0) / (1.0 + s * s),)
        spike_fn.defvjp(_spike_fwd, _spike_bwd)
        key = jax.random.key(seed)
        k1, k2, k3 = jax.random.split(key, 3)
        n_embd = 512
        x = jax.random.normal(k1, (4, 1024, n_embd), dtype=jnp.float32)
        W_fc = jax.random.normal(k2, (4 * n_embd, n_embd), dtype=jnp.float32) / math.sqrt(n_embd)
        W_proj = jax.random.normal(k3, (n_embd, 4 * n_embd), dtype=jnp.float32) / math.sqrt(4 * n_embd)
        return {'x': x, 'W_fc': W_fc, 'W_proj': W_proj}
    _L0_ffn_all = _L0_ffn_setup()
    _L0_ffn_in = {k: v for k, v in _L0_ffn_all.items() if k in ('W_fc', 'W_proj')}
    del _L0_ffn_all
    return {'x': x, 'ctx_1024': ctx_1024, 'g_xattn': g_xattn, 'g_ffn': g_ffn, 'L0_xattn_Wq': _L0_xattn_in['Wq'], 'L0_xattn_Wkv': _L0_xattn_in['Wkv'], 'L0_xattn_Wout': _L0_xattn_in['Wout'], 'L0_xattn_gm': _L0_xattn_in['gm'], 'L0_xattn_bm': _L0_xattn_in['bm'], 'L0_xattn_gl': _L0_xattn_in['gl'], 'L0_xattn_bl': _L0_xattn_in['bl'], 'L0_ffn_W_fc': _L0_ffn_in['W_fc'], 'L0_ffn_W_proj': _L0_ffn_in['W_proj']}

def reference(x, ctx_1024, g_xattn, g_ffn, L0_xattn_Wq, L0_xattn_Wkv, L0_xattn_Wout, L0_xattn_gm, L0_xattn_bm, L0_xattn_gl, L0_xattn_bl, L0_ffn_W_fc, L0_ffn_W_proj):
    import jax
    import jax.numpy as jnp

    def _L0_xattn_ref(x, latents, Wq, Wkv, Wout, gm, bm, gl, bl):
        import jax, jax.numpy as jnp
        import numpy as np
        D_MODEL = 512
        D_HEAD = 64
        NHEADS = 8
        IN_DIM = D_HEAD * NHEADS
        EPS = 1e-05

        def layernorm(x, g, b):
            mu = jnp.mean(x, axis=-1, keepdims=True)
            var = jnp.var(x, axis=-1, keepdims=True)
            return (x - mu) * jax.lax.rsqrt(var + EPS) * g + b
        scale = D_HEAD ** (-0.5)
        xn = layernorm(x, gm, bm)
        ln = layernorm(latents, gl, bl)
        q = ln @ Wq
        kv_input = jnp.concatenate([xn, ln], axis=-2)
        kv = kv_input @ Wkv
        k, v = jnp.split(kv, 2, axis=-1)

        def heads(t):
            B, S, _ = t.shape
            return t.reshape(B, S, NHEADS, D_HEAD).transpose(0, 2, 1, 3)
        q, k, v = (heads(q), heads(k), heads(v))
        q = q / scale
        sim = jnp.einsum('bhid,bhjd->bhij', q, k)
        sim = sim - jax.lax.stop_gradient(jnp.max(sim, axis=-1, keepdims=True))
        attn = jax.nn.softmax(sim, axis=-1)
        out = jnp.einsum('bhij,bhjd->bhid', attn, v)
        B, H, L, dh = out.shape
        out = out.transpose(0, 2, 1, 3).reshape(B, L, H * dh)
        return out @ Wout

    def _L0_ffn_ref(x, W_fc, W_proj):
        import jax, jax.numpy as jnp
        import numpy as np
        import math
        BETA = 0.9
        THRESHOLD = 1.0
        NUM_STEPS = 5
        ALPHA = 2.0

        @jax.custom_vjp
        def spike_fn(u):
            return (u > 0).astype(u.dtype)

        def _spike_fwd(u):
            return (spike_fn(u), u)

        def _spike_bwd(u, g):
            s = jnp.pi / 2.0 * ALPHA * u
            return (g * (ALPHA / 2.0) / (1.0 + s * s),)
        spike_fn.defvjp(_spike_fwd, _spike_bwd)
        h = jnp.square(jax.nn.relu(jnp.einsum('bsd,fd->bsf', x, W_fc)))
        y = jnp.einsum('bsf,df->bsd', h, W_proj)

        def step(mem, _):
            reset = jax.lax.stop_gradient(spike_fn(mem - THRESHOLD))
            mem_new = BETA * mem + y - reset * THRESHOLD
            spk = spike_fn(mem_new - THRESHOLD)
            return (mem_new, spk)
        mem0 = jnp.zeros_like(y)
        _, spks = jax.lax.scan(step, mem0, None, length=NUM_STEPS)
        return jnp.sum(spks, axis=0) / NUM_STEPS
    x = x + jnp.tanh(g_xattn[0]) * _L0_xattn_ref(ctx_1024, _layernorm(x, axis=-1), L0_xattn_Wq, L0_xattn_Wkv, L0_xattn_Wout, L0_xattn_gm, L0_xattn_bm, L0_xattn_gl, L0_xattn_bl)
    x = x + jnp.tanh(g_ffn[0]) * _L0_ffn_ref(_layernorm(x, axis=-1), L0_ffn_W_fc, L0_ffn_W_proj)
    return x

_drawn_inputs = setup_inputs


def setup_inputs(seed=0):
    import zlib

    import numpy as np

    out = dict(_drawn_inputs(seed))
    spreads = {'L0_xattn_gm': (1.0, 0.2),
     'L0_xattn_bm': (0.0, 0.1),
     'L0_xattn_gl': (1.0, 0.2),
     'L0_xattn_bl': (0.0, 0.1)}
    factors = {}
    for name, (base, spread) in spreads.items():
        noise = np.random.default_rng([zlib.crc32(name.encode()), seed]).standard_normal(out[name].shape)
        drawn = base * np.exp(spread * noise) if base else spread * noise
        out[name] = jnp.asarray(drawn.astype(out[name].dtype))
    for name, factor in factors.items():
        out[name] = (out[name] * factor).astype(out[name].dtype)
    return out
```

```python
from contextlib import ExitStack

import concourse.bass as bass
from concourse import mybir

F32 = mybir.dt.float32
F32R = mybir.dt.float32r
BF16 = mybir.dt.bfloat16
ALU = mybir.AluOpType
ACT = mybir.ActivationFunctionType
AX = mybir.AxisListType
RMAX = bass.bass_isa.ReduceOp.max

P = 128
EPS = 1e-5
LOWEST = -3.0e38
BETA = 0.9
THRESHOLD = 1.0
STEPS = 5


def flamingo_block(nc, x, ctx_in, g_xattn, g_ffn, Wq, Wkv, Wout, gm, bm, gl, bl, WfcT, WprojT, out):
    B, L, D = x.shape
    T = ctx_in.shape[1]
    F = WfcT.shape[1]
    DH = 64
    HEADS = D // DH
    DC = D // P
    LT = L // 2
    CTX_TILES = 6
    CT = T // CTX_TILES
    TILES = CTX_TILES + 2
    KEYS = T + L
    HALF = (KEYS // 2 + 1) // 2 * 2
    PAIRS = HEADS // 2
    QSCALE = float(DH) ** 0.5
    ROWS = [CT] * CTX_TILES + [LT] * 2
    AT = [t * CT for t in range(CTX_TILES)] + [T, T + LT]
    BANKS = TILES // 2
    PASSES = ((0, 0), (0, 1), (1, 0))
    TG = 2 * L
    GROUPS = B // 2
    FC = F // P
    assert CT * CTX_TILES == T and CT <= P and HALF <= 512 and D == 512

    x_flat = x.rearrange("b l d -> (b l) d")
    out_flat = out.rearrange("b l d -> (b l) d")
    x1_dram = nc.dram_tensor("x1_scratch", (B * L, D), F32, kind="Internal").ap()

    keep = ExitStack()
    with keep:
        def sb(stack, name, shape, dt=F32):
            return stack.enter_context(nc.sbuf_tensor(name, shape, dt))

        def sem(name):
            return keep.enter_context(nc.semaphore(name))

        ident = sb(keep, "ident", [P, P])
        ident_b = sb(keep, "ident_b", [P, P], BF16)
        ones = sb(keep, "ones", [P, DH])
        gate_in = sb(keep, "gate_in", [P, 2])
        gate = sb(keep, "gate", [P, 2])
        halfneg = sb(keep, "halfneg", [P, 4])
        bn = sb(keep, "bn", [P, 4, 6])
        mv = sb(keep, "mv", [P, 4, 2])
        ve = sb(keep, "ve", [P, 4])
        rstd = sb(keep, "rstd", [P, 4])
        tick = sb(keep, "tick", [P, 3])

        score = keep.enter_context(nc.psum_tensor("score", [P, BANKS, 512], F32))
        work = [keep.enter_context(nc.psum_tensor(f"work{i}", [P, 512], F32)) for i in range(3)]
        heads_out = keep.enter_context(nc.psum_tensor("heads_out", [P, 512], F32))

        a = ExitStack()
        wq = sb(a, "wq", [P, 2, DC, D], F32R)
        wk = sb(a, "wk", [P, 2, DC, D], F32R)
        wv = sb(a, "wv", [P, 2, DC, D], F32R)
        wo = sb(a, "wo", [P, 2, DC, D], F32R)
        affine = sb(a, "affine", [P, 4, DC])
        xin = sb(a, "xin", [P, 4, D])
        xaff = sb(a, "xaff", [P, 2, DC, P])
        xT = sb(a, "xT", [P, 2, DC, KEYS], F32R)
        kst = sb(a, "kst", [P, 2, 2, KEYS], F32R)
        qst = sb(a, "qst", [P, 2, 2, 2, L], F32R)
        vals = sb(a, "vals", [P, TILES, D])
        probs = sb(a, "probs", [P, 4, TILES * L])
        mx = sb(a, "mx", [P, 2, L])
        mxb = sb(a, "mxb", [P, 2, L])
        dpart = sb(a, "dpart", [P, 3, L])
        dlat = sb(a, "dlat", [P, L])
        dsum = sb(a, "dsum", [P, 4, L])
        rden = sb(a, "rden", [P, L])
        on32 = sb(a, "on32", [P, L])
        oT = sb(a, "oT", [P, 2, PAIRS, L], F32R)
        xres = sb(a, "xres", [P, 2, D])
        a.close()

        bb = ExitStack()
        wf = sb(bb, "wf", [P, 2, FC, DC * P], F32R)
        wp = sb(bb, "wp", [P, 2, FC, D], F32R)
        zt = sb(bb, "zt", [P, 4, D])
        fin = sb(bb, "fin", [P, 4, D])
        zT = sb(bb, "zT", [P, 2, DC, TG], F32R)
        relu = sb(bb, "relu", [P, 2, TG])
        h32 = sb(bb, "h32", [P, 2, TG])
        hT = sb(bb, "hT", [P, 3, 2, TG], F32R)
        neuron = sb(bb, "neuron", [P, 4096])
        spikes = sb(bb, "spikes", [P, DC * TG], BF16)
        bb.close()

        ident_ready = sem("ident_ready")
        const_ready = sem("const_ready")
        small_in = sem("small_in")
        gate_ready = sem("gate_ready")
        gate_half = sem("gate_half")
        w_in = [sem(f"w_in{i}") for i in range(4)]
        w_hi = sem("w_hi")
        w_lo = sem("w_lo")
        pad_ready = sem("pad_ready")
        x_in = [sem(f"x_in{i}") for i in range(4)]
        bn_done = sem("bn_done")
        mv_done = sem("mv_done")
        ve_done = sem("ve_done")
        rstd_done = sem("rstd_done")
        ln_half = sem("ln_half")
        ln_done = sem("ln_done")
        tr_done = sem("tr_done")
        aff_done = sem("aff_done")
        xhi_done = sem("xhi_done")
        xlo_done = sem("xlo_done")
        kq_mm = sem("kq_mm")
        kq_hi = sem("kq_hi")
        kq_done = sem("kq_done")
        v_mm = sem("v_mm")
        v_done = sem("v_done")
        s_mm = sem("s_mm")
        s_copied = sem("s_copied")
        max_done = sem("max_done")
        maxb_done = sem("maxb_done")
        sub_done = sem("sub_done")
        exp_done = sem("exp_done")
        dpart_done = sem("dpart_done")
        dsum_done = sem("dsum_done")
        pv_done = sem("pv_done")
        rden_done = sem("rden_done")
        on_done = sem("on_done")
        ohi_done = sem("ohi_done")
        o_done = sem("o_done")
        wo_mm = sem("wo_mm")
        x1_done = sem("x1_done")
        res_in = [sem(f"res_in{i}") for i in range(2)]
        x1_out = [sem(f"x1_out{i}") for i in range(2)]
        fw_in = [sem(f"fw_in{i}") for i in range(4)]
        fw_hi = sem("fw_hi")
        fw_lo = sem("fw_lo")
        zt_in = sem("zt_in")
        fin_in = sem("fin_in")
        g_bn = sem("g_bn")
        g_mv = sem("g_mv")
        g_ve = sem("g_ve")
        g_rstd = sem("g_rstd")
        z_done = sem("z_done")
        zt_mm = sem("zt_mm")
        z_hi = sem("z_hi")
        z_lo = sem("z_lo")
        up_mm = sem("up_mm")
        relu_done = sem("relu_done")
        h_done = sem("h_done")
        h_hi = sem("h_hi")
        h_lo = sem("h_lo")
        down_mm = sem("down_mm")
        y_mm = sem("y_mm")
        y_done = sem("y_done")
        lif = sem("lif")
        spk_done = sem("spk_done")
        spkT_mm = sem("spkT_mm")
        fin_done = sem("fin_done")
        fin_out = sem("fin_out")

        block = keep.enter_context(nc.Block())

        def tile_src(b, t):
            if t < CTX_TILES:
                return ctx_in[b, AT[t]:AT[t] + CT, :]
            return x[b, (t - CTX_TILES) * LT:(t - CTX_TILES + 1) * LT, :]

        NA = B
        LIF_OPS = 24

        @block.sync
        def _(sp):
            def load_tile(b, t):
                sp.dma_start(xin[0:ROWS[t], t % 4, :], tile_src(b, t)).then_inc(x_in[t % 4], 16)

            def load_residual(b, i):
                sp.dma_start(xres[0:LT, i, :], x[b, i * LT:(i + 1) * LT, :]).then_inc(res_in[i], 16)

            def refill(b, last):
                for t in range(TILES):
                    sp.wait_ge(tr_done, b * TILES + (t + 1))
                    if t < 4:
                        load_tile(b, t + 4)
                    elif not last:
                        load_tile(b + 1, t - 4)

            def residual(b, last):
                for i in range(2):
                    sp.wait_ge(x1_done, b * 2 + (i + 1))
                    rows = x1_dram.rearrange("(b i r) d -> b i r d", b=B, i=2)[b, i]
                    sp.dma_start(rows, xres[0:LT, i, :]).then_inc(x1_out[i], 16)
                    sp.wait_ge(x1_out[i], b * 16 + 16)
                    if not last:
                        load_residual(b + 1, i)

            for t in range(4):
                load_tile(0, t)
            sp.dma_start(gate_in[:, 0:1], g_xattn).then_inc(small_in, 16)
            sp.dma_start(gate_in[:, 1:2], g_ffn).then_inc(small_in, 16)
            for i, v in enumerate((gm, bm, gl, bl)):
                sp.dma_start(affine[:, i, :], v).then_inc(small_in, 16)
            for i, w in enumerate((Wkv[:, 0:D], Wq, Wkv[:, D:2 * D], Wout)):
                w_chunks = w.rearrange("(k p) n -> p k n", p=P)
                if i < 2:
                    sp.dma_start(vals[:, 4 * i:4 * i + DC, :], w_chunks).then_inc(w_in[i], 16)
                else:
                    sp.wait_ge(w_lo, i - 1)
                    sp.dma_start(vals[:, 4 * (i - 2):4 * (i - 2) + DC, :], w_chunks).then_inc(w_in[i], 16)
            for i in range(2):
                load_residual(0, i)
            refill(0, False)
            with sp.Fori(1, NA - 1) as b:
                refill(b, False)
                residual(b - 1, False)
            refill(NA - 1, True)
            residual(NA - 2, False)
            residual(NA - 1, True)

            def group_rows(d, g):
                return d.rearrange("(g i r) d -> g r i d", g=GROUPS, i=4)[g]

            def load_z(g):
                sp.dma_start(zt[0:LT, :, :], group_rows(x1_dram, g)).then_inc(zt_in, 16)

            def load_fin(g):
                sp.dma_start(fin[0:LT, :, :], group_rows(x1_dram, g)).then_inc(fin_in, 16)

            def store_fin(g):
                for i in range(4):
                    sp.wait_ge(fin_done, g * 4 + (i + 1))
                    rows = out_flat.rearrange("(g i r) d -> g i r d", g=GROUPS, i=4)[g, i]
                    sp.dma_start(rows, fin[0:LT, i, :]).then_inc(fin_out, 16)
                sp.wait_ge(fin_out, g * 64 + 64)

            def group(g, last):
                if not last:
                    sp.wait_ge(zt_mm, g * 4 + 4)
                    load_z(g + 1)
                store_fin(g - 1)
                load_fin(g)

            load_z(0)
            for j in range(FC):
                if j >= 4:
                    sp.wait_ge(fw_lo, j - 3)
                stage = neuron[:, (j % 4) * 1024:(j % 4 + 1) * 1024]
                sp.dma_start(stage[:, 0:512].rearrange("p (k f) -> p k f", k=DC),
                             WfcT.rearrange("(k p) (j f) -> j p k f", p=P, f=P)[j]).then_inc(fw_in[j % 4], 16)
                sp.dma_start(stage[:, 512:1024], WprojT[j * P:(j + 1) * P, :]).then_inc(fw_in[j % 4], 16)
            load_fin(0)
            sp.wait_ge(zt_mm, 4)
            load_z(1)
            with sp.Fori(1, GROUPS - 1) as g:
                group(g, False)
            group(GROUPS - 1, True)
            store_fin(GROUPS - 1)

        @block.tensor
        def _(pe):
            def product(bank, lhs, rhs, chunks, passes=PASSES):
                n = 0
                for i, j in passes:
                    for k in range(chunks):
                        mm = pe.matmul(bank, lhs(i, k), rhs(j, k), start=(n == 0),
                                       stop=(n == len(passes) * chunks - 1))
                        n += 1
                return mm

            def transposes(b, t, first):
                if t < 3:
                    if not first:
                        pe.wait_ge(kq_done, b * 12 - 2 + t)
                else:
                    pe.wait_ge(aff_done, b * TILES + (t - 2))
                pe.wait_ge(ln_done, b * TILES + (t + 1))
                bank = work[(t + 2) % 3]
                for k in range(DC):
                    mm = pe.transpose(bank[:, k * P:k * P + ROWS[t]], xin[0:ROWS[t], t % 4, k * P:(k + 1) * P],
                                      ident[0:ROWS[t], 0:ROWS[t]])
                mm.then_inc(tr_done, 1)

            def keys_queries(b, c):
                cols = slice(c * P, (c + 1) * P)
                for u in range(3):
                    if c == 0:
                        pe.wait_ge(aff_done, b * TILES + (6 + u))
                        if u == 0:
                            pe.wait_ge(xhi_done, b * TILES + TILES)
                            pe.wait_ge(xlo_done, b * TILES + TILES)
                    elif c == 1:
                        pe.wait_ge(kq_done, b * 12 + 3)
                        if u > 0:
                            pe.wait_ge(x1_done, b * 2)
                    elif c == 2:
                        pe.wait_ge(v_done, b * TILES + (6 + u))
                    else:
                        pe.wait_ge(kq_done, b * 12 + (7 + u))
                    bank = work[((25, 0, 11, 14)[c] + u) % 3]
                    if u < 2:
                        lo, hi = (0, HALF) if u == 0 else (HALF, KEYS)
                        mm = product(bank[:, 0:hi - lo], lambda i, k: wk[:, i, k, cols],
                                     lambda i, k: xT[:, i, k, lo:hi], DC)
                    else:
                        mm = product(bank[:, 0:L], lambda i, k: wq[:, i, k, cols],
                                     lambda i, k: xT[:, i, k, T:KEYS], DC)
                    mm.then_inc(kq_mm, 1)

            def values(b):
                for t in range(TILES):
                    if t < 3:
                        pe.wait_ge(kq_done, b * 12 + (4 + t))
                    else:
                        pe.wait_ge(v_done, b * TILES + (t - 2))
                    product(work[t % 3][0:ROWS[t], :], lambda i, k: xT[:, i, k, AT[t]:AT[t] + ROWS[t]],
                            lambda i, k: wv[:, i, k, :], DC).then_inc(v_mm, 1)

            def scores(b, h):
                s, e = h // 2 % 2, h % 2
                pe.wait_ge(kq_done, b * 12 + (3 * (h // 2) + 3))
                for t in range(TILES):
                    if t % 2 == 0:
                        pe.wait_ge(s_copied, (b * HEADS + h) * BANKS - (BANKS - 1 - t // 2 if h else 0))
                    for j in range(2):
                        mm = pe.matmul(score[0:ROWS[t], t // 2, t % 2 * L:(t % 2 + 1) * L],
                                       kst[:, s, e, AT[t]:AT[t] + ROWS[t]], qst[:, s, j, e, :],
                                       start=(j == 0), stop=(j == 1))
                    if t % 2:
                        mm.then_inc(s_mm, 1)

            def attend(b, p):
                pe.wait_ge(v_done, b * TILES + TILES)
                pe.wait_ge(o_done, b * PAIRS + p)
                pe.wait_ge(exp_done, b * HEADS + (2 * p + 2))
                for t in range(TILES):
                    for e in range(2):
                        h = 2 * p + e
                        pe.matmul(heads_out[e * DH:(e + 1) * DH, 0:L], vals[0:ROWS[t], t, h * DH:(h + 1) * DH],
                                  probs[0:ROWS[t], h % 4, t * L:(t + 1) * L],
                                  start=(t == 0), stop=(t == TILES - 1))
                pe.wait_ge(dsum_done, b * HEADS + (2 * p + 2))
                for e in range(2):
                    mm = pe.matmul(heads_out[e * DH:(e + 1) * DH, L:2 * L], ones[0:CT, :],
                                   dsum[0:CT, (2 * p + e) % 4, :], start=True, stop=True)
                mm.then_inc(pv_done, 1)

            def out_projection(b, last):
                pe.wait_ge(o_done, b * PAIRS + PAIRS)
                for i in range(2):
                    pe.wait_ge(kq_done, b * 12 + (12 if last else 13 + i))
                    product(work[(28 + i) % 3][0:LT, :], lambda m, k: oT[:, m, k, i * LT:(i + 1) * LT],
                            lambda m, k: wo[:, m, k, :], DC).then_inc(wo_mm, 1)

            def batch(b, last):
                scores(b, 0)
                scores(b, 1)
                keys_queries(b, 1)
                scores(b, 2)
                scores(b, 3)
                values(b)
                keys_queries(b, 2)
                attend(b, 0)
                scores(b, 4)
                scores(b, 5)
                keys_queries(b, 3)
                if not last:
                    for t in range(4):
                        transposes(b + 1, t, False)
                attend(b, 1)
                scores(b, 6)
                scores(b, 7)
                if not last:
                    for t in range(4, TILES):
                        transposes(b + 1, t, False)
                attend(b, 2)
                if not last:
                    keys_queries(b + 1, 0)
                attend(b, 3)
                out_projection(b, last)

            pe.wait_ge(ident_ready, 4)
            pe.wait_ge(const_ready, 1)
            for t in range(TILES):
                transposes(0, t, True)
            pe.wait_ge(w_lo, 2)
            keys_queries(0, 0)
            pe.wait_ge(w_lo, 4)
            with pe.Fori(0, NA - 1) as b:
                batch(b, False)
            batch(NA - 1, True)

            def group_transposes(g, first):
                for i in range(4):
                    pe.wait_ge(z_done, g * 4 + (i + 1))
                    if i >= 2:
                        pe.wait_ge(z_lo, g * 4 + (i - 1))
                    elif not first:
                        pe.wait_ge(fin_done, g * 4 - 4)
                    bank = (work[2], heads_out)[i % 2]
                    for k in range(DC):
                        mm = pe.transpose(bank[:, k * LT:(k + 1) * LT], zt[0:LT, i, k * P:(k + 1) * P],
                                          ident[0:LT, 0:LT])
                    mm.then_inc(zt_mm, 1)

            def up(g, j):
                if j < 2:
                    pe.wait_ge(relu_done, g * FC)
                else:
                    pe.wait_ge(relu_done, g * FC + (j - 1))
                pe.wait_ge(fw_lo, j + 1)
                product(work[j % 2][:, 0:TG], lambda i, k: wf[:, i, j, k * P:(k + 1) * P],
                        lambda i, k: zT[:, i, k, :], DC).then_inc(up_mm, 1)

            def down(g, j):
                pe.wait_ge(h_lo, g * FC + (j + 1))
                if j == 0:
                    pe.wait_ge(y_done, g * DC)
                for d in range(DC):
                    for n, (w, a_) in enumerate(PASSES):
                        mm = pe.matmul(score[:, d, 0:TG], wp[:, w, j, d * P:(d + 1) * P], hT[:, j % 3, a_, :],
                                       start=(j == 0 and n == 0), stop=(j == FC - 1 and n == 2))
                    if j == FC - 1:
                        mm.then_inc(y_mm, 1)
                    elif d == DC - 1:
                        mm.then_inc(down_mm, 1)

            def spikes_back(g):
                pe.wait_ge(spk_done, g * 2 + 2)
                for i in range(4):
                    if i >= 2:
                        pe.wait_ge(fin_done, g * 4 + (i - 1))
                    bank = (work[2], heads_out)[i % 2][:, 0:D // 2].bitcast(BF16)
                    for k in range(DC):
                        mm = pe.transpose(bank[0:LT, k * P:(k + 1) * P],
                                          spikes[:, k * TG + i * LT:k * TG + (i + 1) * LT], ident_b[:, :])
                    mm.then_inc(spkT_mm, 1)

            def group(g, first):
                group_transposes(g, first)
                pe.wait_ge(z_lo, g * 4 + 4)
                for j in range(FC):
                    up(g, j)
                    if j >= 2:
                        down(g, j - 2)
                    if j == FC - 2 and not first:
                        spikes_back(g - 1)
                down(g, FC - 2)
                down(g, FC - 1)

            group(0, True)
            with pe.Fori(1, GROUPS) as g:
                group(g, False)
            spikes_back(GROUPS - 1)

        @block.scalar
        def _(act):
            def copy_scores(b, h):
                act.wait_ge(pv_done, b * PAIRS + max(h // 2 - 1, 0))
                for k in range(BANKS):
                    act.wait_ge(s_mm, (b * HEADS + h) * BANKS + (k + 1))
                    r = ROWS[2 * k]
                    act.activation(probs[0:r, h % 4, 2 * k * L:(2 * k + 2) * L], score[0:r, k, 0:2 * L],
                                   ACT.Copy).then_inc(s_copied, 1)

            def exponentials(b, h):
                act.wait_ge(sub_done, (b * HEADS + h) * 2 + 2)
                act.activation(probs[0:CT, h % 4, 0:CTX_TILES * L], probs[0:CT, h % 4, 0:CTX_TILES * L], ACT.Exp)
                act.activation(probs[0:LT, h % 4, CTX_TILES * L:], probs[0:LT, h % 4, CTX_TILES * L:],
                               ACT.Exp).then_inc(exp_done, 1)

            def kq_hi_parts(b, c):
                s = c % 2
                if c == 1:
                    act.wait_ge(s_mm, b * HEADS * BANKS)
                elif c >= 2:
                    act.wait_ge(s_mm, b * HEADS * BANKS + (2 * c - 2) * BANKS)
                for u in range(3):
                    act.wait_ge(kq_mm, b * 12 + (3 * c + u + 1))
                    bank = work[((25, 0, 11, 14)[c] + u) % 3]
                    for e in range(2):
                        rows = slice(e * DH, (e + 1) * DH)
                        if u < 2:
                            lo, hi = (0, HALF) if u == 0 else (HALF, KEYS)
                            act.activation(kst[rows, s, e, lo:hi], bank[rows, 0:hi - lo],
                                           ACT.Copy).then_inc(kq_hi, 1)
                        else:
                            act.activation(qst[0:DH, s, 0, e, :], bank[rows, 0:L], ACT.Copy, scale=QSCALE)
                            act.activation(qst[DH:P, s, 0, e, :], bank[rows, 0:L], ACT.Copy,
                                           scale=QSCALE).then_inc(kq_hi, 1)

            def copy_values(b, ts):
                act.wait_ge(pv_done, b * PAIRS)
                for t in ts:
                    act.wait_ge(v_mm, b * TILES + (t + 1))
                    act.activation(vals[0:ROWS[t], t, :], work[t % 3][0:ROWS[t], :], ACT.Copy).then_inc(v_done, 1)

            def affine_tile(b, t):
                act.wait_ge(tr_done, b * TILES + (t + 1))
                if t < 2:
                    act.wait_ge(xlo_done, b * TILES)
                else:
                    act.wait_ge(xlo_done, b * TILES + (t - 1))
                g = 0 if t < CTX_TILES else 2
                for k in range(DC):
                    ins = act.activation(xaff[:, t % 2, k, 0:ROWS[t]], work[(t + 2) % 3][:, k * P:k * P + ROWS[t]],
                                         ACT.Identity, scale=affine[:, g, k:k + 1], bias=affine[:, g + 1, k:k + 1])
                ins.then_inc(aff_done, 1)

            def batch(b, last):
                copy_scores(b, 0)
                copy_scores(b, 1)
                kq_hi_parts(b, 1)
                exponentials(b, 0)
                copy_scores(b, 2)
                exponentials(b, 1)
                copy_scores(b, 3)
                copy_values(b, range(0, 3))
                exponentials(b, 2)
                copy_values(b, range(3, 6))
                exponentials(b, 3)
                copy_values(b, range(6, 8))
                kq_hi_parts(b, 2)
                copy_scores(b, 4)
                copy_scores(b, 5)
                kq_hi_parts(b, 3)
                exponentials(b, 4)
                if not last:
                    affine_tile(b + 1, 0)
                    affine_tile(b + 1, 1)
                exponentials(b, 5)
                if not last:
                    affine_tile(b + 1, 2)
                    affine_tile(b + 1, 3)
                copy_scores(b, 6)
                copy_scores(b, 7)
                if not last:
                    affine_tile(b + 1, 4)
                    affine_tile(b + 1, 5)
                exponentials(b, 6)
                if not last:
                    affine_tile(b + 1, 6)
                    affine_tile(b + 1, 7)
                exponentials(b, 7)
                if not last:
                    kq_hi_parts(b + 1, 0)

            act.wait_ge(small_in, 96)
            act.activation(gate[:, :], gate_in[:, :], ACT.Tanh).then_inc(gate_half, 1)
            for i, w in enumerate((wk, wq, wv, wo)):
                act.wait_ge(w_in[i], 16)
                s = 4 * (i % 2)
                act.activation(w[:, 0], vals[:, s:s + DC, :], ACT.Copy).then_inc(w_hi, 1)
                if i == 1:
                    for t in range(TILES):
                        affine_tile(0, t)
            kq_hi_parts(0, 0)
            act.wait_ge(w_lo, 4)
            act.wait_ge(pad_ready, 2)
            with act.Fori(0, NA - 1) as b:
                batch(b, False)
            batch(NA - 1, True)

            def split_weights(j):
                act.wait_ge(fw_in[j % 4], 32 * (j // 4 + 1))
                stage = neuron[:, (j % 4) * 1024:(j % 4 + 1) * 1024]
                act.activation(wf[:, 0, j, :], stage[:, 0:512], ACT.Copy)
                act.activation(wp[:, 0, j, :], stage[:, 512:1024], ACT.Copy).then_inc(fw_hi, 1)

            def group(g, first):
                for i in range(4):
                    act.wait_ge(zt_mm, g * 4 + (i + 1))
                    act.activation(zT[:, 0, :, i * LT:(i + 1) * LT],
                                   (work[2], heads_out)[i % 2][:, 0:TG].rearrange("p (k r) -> p k r", k=DC),
                                   ACT.Copy).then_inc(z_hi, 1)
                if first:
                    split_weights(0)
                    split_weights(1)
                for j in range(FC):
                    act.wait_ge(up_mm, g * FC + (j + 1))
                    if j < 2:
                        act.wait_ge(h_done, g * FC)
                    else:
                        act.wait_ge(h_done, g * FC + (j - 1))
                    act.activation(relu[:, j % 2, :], work[j % 2][:, 0:TG], ACT.Relu).then_inc(relu_done, 1)
                    act.wait_ge(h_done, g * FC + (j + 1))
                    if j < 3:
                        act.wait_ge(y_mm, g * DC)
                    else:
                        act.wait_ge(down_mm, g * (FC - 1) + (j - 2))
                    act.activation(hT[:, j % 3, 0, :], h32[:, j % 2, :], ACT.Copy).then_inc(h_hi, 1)
                    if first and j + 2 < FC:
                        split_weights(j + 2)
                act.wait_ge(spk_done, g * 2)
                act.wait_ge(fw_lo, FC)
                for d in range(DC):
                    act.wait_ge(y_mm, g * DC + (d + 1))
                    act.activation(neuron[:, d * TG:(d + 1) * TG], score[:, d, 0:TG], ACT.Copy).then_inc(y_done, 1)

            group(0, True)
            with act.Fori(1, GROUPS) as g:
                group(g, False)

        @block.vector
        def _(dve):
            def scale_max(b, h):
                dve.wait_ge(s_copied, (b * HEADS + h + 1) * BANKS)
                dve.wait_ge(maxb_done, b * HEADS + max(h - 1, 0))
                dve.tensor_reduce(mx[0:CT, h % 2, :],
                                  probs[0:CT, h % 4, :].rearrange("p (t l) -> p l t", t=TILES),
                                  AX.X, ALU.max).then_inc(max_done, 1)

            def subtract(b, h):
                dve.wait_ge(maxb_done, b * HEADS + (h + 1))
                for r, lo, n in ((CT, 0, CTX_TILES), (LT, CTX_TILES, 2)):
                    v = probs[0:r, h % 4, lo * L:(lo + n) * L].rearrange("p (t l) -> p t l", t=n)
                    dve.tensor_tensor(v, v, mxb[0:r, h % 2:h % 2 + 1, :].to_broadcast([r, n, L]),
                                      ALU.subtract).then_inc(sub_done, 1)

            def kq_lo_parts(b, c):
                s = c % 2
                for u in range(3):
                    bank = work[((25, 0, 11, 14)[c] + u) % 3]
                    for e in range(2):
                        rows = slice(e * DH, (e + 1) * DH)
                        other = slice((1 - e) * DH, (2 - e) * DH)
                        dve.wait_ge(kq_hi, (b * 12 + (3 * c + u)) * 2 + (e + 1))
                        if u < 2:
                            lo, hi = (0, HALF) if u == 0 else (HALF, KEYS)
                            ins = dve.tensor_tensor(kst[other, s, e, lo:hi], bank[rows, 0:hi - lo],
                                                    kst[rows, s, e, lo:hi].bitcast(F32), ALU.subtract)
                        else:
                            for r in (slice(0, DH), slice(DH, P)):
                                ins = dve.scalar_tensor_tensor(qst[r, s, 1, e, :], bank[rows, 0:L], QSCALE,
                                                               qst[rows, s, 0, e, :].bitcast(F32),
                                                               ALU.mult, ALU.subtract)
                    ins.then_inc(kq_done, 1)

            def normalise(b, p):
                dve.wait_ge(pv_done, b * PAIRS + (p + 1))
                n = b * PAIRS + p
                dve.reciprocal(rden[:, :], heads_out[:, L:2 * L]).then_inc(rden_done, 1)
                dve.wait_ge(rden_done, n + 1)
                dve.tensor_tensor(on32[:, :], heads_out[:, 0:L], rden[:, :], ALU.mult).then_inc(on_done, 1)
                dve.wait_ge(on_done, n + 1)
                dve.wait_ge(wo_mm, b * 2)
                dve.tensor_copy(oT[:, 0, p, :], on32[:, :]).then_inc(ohi_done, 1)
                dve.wait_ge(ohi_done, n + 1)
                dve.tensor_tensor(oT[:, 1, p, :], on32[:, :], oT[:, 0, p, :].bitcast(F32),
                                  ALU.subtract).then_inc(o_done, 1)

            GOES = ([0, 1, 2, 3], [4, 5, 6, 7], [6, 7])
            BEFORE = (0, 4, 8)

            def statistics(b, go):
                n0 = b * 10 + BEFORE[go]
                for i, t in enumerate(GOES[go]):
                    r = ROWS[t]
                    if go < 2:
                        dve.wait_ge(x_in[t % 4], b * 32 + 16 * (t // 4 + 1))
                    else:
                        dve.wait_ge(ln_half, b * 2 + (i + 1))
                    dve.bn_stats(bn[0:r, i, :], xin[0:r, t % 4, :]).then_inc(bn_done, 1)
                dve.wait_ge(bn_done, n0 + len(GOES[go]))
                dve.tensor_copy(tick[:, 0:1], halfneg[:, 0:1])
                for i, t in enumerate(GOES[go]):
                    r = ROWS[t]
                    dve.bn_aggr(mv[0:r, i, :], bn[0:r, i, :]).then_inc(mv_done, 1)
                n = len(GOES[go])
                dve.wait_ge(mv_done, n0 + n)
                dve.tensor_scalar(ve[:, 0:n], mv[:, 0:n, 1], EPS, None, ALU.add).then_inc(ve_done, 1)

            def centre(b, go):
                dve.wait_ge(rstd_done, b * 3 + (go + 1))
                for i, t in enumerate(GOES[go]):
                    r = ROWS[t]
                    ins = dve.tensor_scalar(xin[0:r, t % 4, :], xin[0:r, t % 4, :], mv[0:r, i, 0:1],
                                            rstd[0:r, i:i + 1], ALU.subtract, ALU.mult)
                    ins.then_inc(ln_half if go == 1 and t >= CTX_TILES else ln_done, 1)

            def hi_tile(b, t):
                if t == 0:
                    dve.wait_ge(kq_mm, b * 12)
                dve.wait_ge(aff_done, b * TILES + (t + 1))
                dve.tensor_copy(xT[:, 0, :, AT[t]:AT[t] + ROWS[t]],
                                xaff[:, t % 2, :, 0:ROWS[t]]).then_inc(xhi_done, 1)

            def gated_residual(b):
                for i in range(2):
                    dve.wait_ge(wo_mm, b * 2 + (i + 1))
                    dve.wait_ge(res_in[i], b * 16 + 16)
                    dve.scalar_tensor_tensor(xres[0:LT, i, :], work[(28 + i) % 3][0:LT, :], gate[0:LT, 0:1],
                                             xres[0:LT, i, :], ALU.mult, ALU.add).then_inc(x1_done, 1)

            def batch(b, last):
                scale_max(b, 0)
                scale_max(b, 1)
                subtract(b, 0)
                kq_lo_parts(b, 1)
                subtract(b, 1)
                scale_max(b, 2)
                scale_max(b, 3)
                subtract(b, 2)
                if not last:
                    statistics(b + 1, 0)
                subtract(b, 3)
                if not last:
                    centre(b + 1, 0)
                kq_lo_parts(b, 2)
                normalise(b, 0)
                scale_max(b, 4)
                scale_max(b, 5)
                subtract(b, 4)
                kq_lo_parts(b, 3)
                subtract(b, 5)
                if not last:
                    for t in range(4):
                        hi_tile(b + 1, t)
                normalise(b, 1)
                if not last:
                    statistics(b + 1, 1)
                scale_max(b, 6)
                if not last:
                    centre(b + 1, 1)
                    statistics(b + 1, 2)
                scale_max(b, 7)
                subtract(b, 6)
                if not last:
                    centre(b + 1, 2)
                    for t in range(4, 6):
                        hi_tile(b + 1, t)
                subtract(b, 7)
                if not last:
                    for t in range(6, TILES):
                        hi_tile(b + 1, t)
                normalise(b, 2)
                if not last:
                    kq_lo_parts(b + 1, 0)
                normalise(b, 3)
                gated_residual(b)

            dve.memset(ones[:, :], 1.0).then_inc(const_ready, 1)
            dve.memset(halfneg[:, :], -0.5).then_inc(const_ready, 1)
            dve.memset(mv[:, :, :], 1.0).then_inc(const_ready, 1)
            dve.memset(mx[:, :, :], LOWEST).then_inc(pad_ready, 1)
            dve.memset(probs[64:P, :, CTX_TILES * L:], LOWEST).then_inc(pad_ready, 1)
            dve.wait_ge(const_ready, 3)
            dve.wait_ge(pad_ready, 2)
            statistics(0, 0)
            centre(0, 0)
            for i, w in enumerate((wk, wq)):
                dve.wait_ge(w_hi, i + 1)
                dve.tensor_tensor(w[:, 1], vals[:, 4 * i:4 * i + DC, :], w[:, 0].bitcast(F32),
                                  ALU.subtract).then_inc(w_lo, 1)
            for t in range(4):
                hi_tile(0, t)
            statistics(0, 1)
            centre(0, 1)
            statistics(0, 2)
            centre(0, 2)
            for t in range(4, TILES):
                hi_tile(0, t)
            dve.wait_ge(gate_half, 1)
            dve.tensor_scalar(gate[:, 1:2], gate[:, 1:2], 1.0 / STEPS, None, ALU.mult).then_inc(gate_ready, 1)
            for i, w in enumerate((wv, wo)):
                dve.wait_ge(w_hi, i + 3)
                dve.tensor_tensor(w[:, 1], vals[:, 4 * i:4 * i + DC, :], w[:, 0].bitcast(F32),
                                  ALU.subtract).then_inc(w_lo, 1)
            kq_lo_parts(0, 0)
            with dve.Fori(0, NA - 1) as b:
                batch(b, False)
            batch(NA - 1, True)

            def group_statistics(g):
                dve.wait_ge(zt_in, g * 16 + 16)
                for i in range(4):
                    dve.bn_stats(bn[0:LT, i, :], zt[0:LT, i, :]).then_inc(g_bn, 1)
                dve.wait_ge(g_bn, g * 4 + 4)
                dve.tensor_copy(tick[:, 0:1], halfneg[:, 0:1])
                for i in range(4):
                    dve.bn_aggr(mv[0:LT, i, :], bn[0:LT, i, :]).then_inc(g_mv, 1)
                dve.wait_ge(g_mv, g * 4 + 4)
                dve.tensor_scalar(ve[:, 0:4], mv[:, 0:4, 1], EPS, None, ALU.add).then_inc(g_ve, 1)

            def group_centre(g):
                dve.wait_ge(g_rstd, g + 1)
                for i in range(4):
                    dve.tensor_scalar(zt[0:LT, i, :], zt[0:LT, i, :], mv[0:LT, i, 0:1], rstd[0:LT, i:i + 1],
                                      ALU.subtract, ALU.mult).then_inc(z_done, 1)

            def split_weights(j):
                stage = neuron[:, (j % 4) * 1024:(j % 4 + 1) * 1024]
                dve.wait_ge(fw_hi, j + 1)
                dve.tensor_tensor(wf[:, 1, j, :], stage[:, 0:512], wf[:, 0, j, :].bitcast(F32), ALU.subtract)
                dve.tensor_tensor(wp[:, 1, j, :], stage[:, 512:1024], wp[:, 0, j, :].bitcast(F32),
                                  ALU.subtract).then_inc(fw_lo, 1)

            W = DC * TG // 2
            cur = neuron[:, 2 * W:3 * W]
            nxt = neuron[:, 3 * W:4 * W]

            def neuron_op(g, n):
                half, k = n // 13, n % 13
                y = neuron[:, half * W:(half + 1) * W]
                s = spikes[:, half * W:(half + 1) * W]
                if n == 0:
                    dve.wait_ge(y_done, g * DC + DC)
                    dve.wait_ge(spkT_mm, g * 4)
                dve.wait_ge(lif, g * LIF_OPS + n - half)
                if n == 13:
                    dve.wait_ge(spk_done, g * 2 + 1)
                if k == 0:
                    ins = dve.tensor_scalar(s, y, THRESHOLD, None, ALU.is_gt)
                elif k == 1:
                    ins = dve.scalar_tensor_tensor(nxt, y, BETA, y, ALU.mult, ALU.add)
                elif k == 2:
                    ins = dve.scalar_tensor_tensor(cur, y, THRESHOLD, nxt, ALU.is_gt, ALU.subtract)
                elif k % 3 == 0:
                    ins = dve.scalar_tensor_tensor(s, cur, -THRESHOLD, s, ALU.is_lt, ALU.add)
                elif k % 3 == 1:
                    ins = dve.scalar_tensor_tensor(nxt, cur, -BETA, y, ALU.mult, ALU.add)
                else:
                    ins = dve.scalar_tensor_tensor(cur, cur, -THRESHOLD, nxt, ALU.is_lt, ALU.subtract)
                ins.then_inc(spk_done if k == 12 else lif, 1)

            def finish(g):
                dve.wait_ge(fin_in, g * 16 + 16)
                for i in range(4):
                    dve.wait_ge(spkT_mm, g * 4 + (i + 1))
                    bank = (work[2], heads_out)[i % 2][:, 0:D // 2].bitcast(BF16)
                    dve.scalar_tensor_tensor(fin[0:LT, i, :], bank[0:LT, :], gate[0:LT, 1:2],
                                             fin[0:LT, i, :], ALU.mult, ALU.add).then_inc(fin_done, 1)

            def group(g, first, last):
                for i in range(4):
                    dve.wait_ge(z_hi, g * 4 + (i + 1))
                    dve.tensor_tensor(zT[:, 1, :, i * LT:(i + 1) * LT],
                                      (work[2], heads_out)[i % 2][:, 0:TG].rearrange("p (k r) -> p k r", k=DC),
                                      zT[:, 0, :, i * LT:(i + 1) * LT].bitcast(F32),
                                      ALU.subtract).then_inc(z_lo, 1)
                if first:
                    split_weights(0)
                    split_weights(1)
                for j in range(FC):
                    dve.wait_ge(h_hi, g * FC + (j + 1))
                    dve.tensor_tensor(hT[:, j % 3, 1, :], h32[:, j % 2, :], hT[:, j % 3, 0, :].bitcast(F32),
                                      ALU.subtract).then_inc(h_lo, 1)
                    if first and j + 2 < FC:
                        split_weights(j + 2)
                    if not first and j < 13:
                        neuron_op(g - 1, 2 * j)
                        neuron_op(g - 1, 2 * j + 1)
                    if not last and j == 13:
                        group_statistics(g + 1)
                    if not last and j == 14:
                        group_centre(g + 1)
                    if not first and j == 14:
                        finish(g - 1)

            group_statistics(0)
            group_centre(0)
            group(0, True, False)
            with dve.Fori(1, GROUPS - 1) as g:
                group(g, False, False)
            group(GROUPS - 1, False, True)
            for n in range(26):
                neuron_op(GROUPS - 1, n)
            finish(GROUPS - 1)

        @block.gpsimd
        def _(pool):
            def all_max(b, h):
                pool.wait_ge(max_done, b * HEADS + (h + 1))
                pool.wait_ge(sub_done, (b * HEADS + max(h - 1, 0)) * 2)
                pool.tensor_tensor(tick[:, 1 + h % 2:2 + h % 2], halfneg[:, 0:1], halfneg[:, 0:1], ALU.mult)
                pool.partition_all_reduce(mxb[:, h % 2, :], mx[:, h % 2, :], P, RMAX).then_inc(maxb_done, 1)

            def denominators(b, h):
                p = probs[:, h % 4, :].rearrange("p (t l) -> p t l", t=TILES)
                n = (b * HEADS + h) * 4
                pool.wait_ge(exp_done, b * HEADS + (h + 1))
                pool.wait_ge(dsum_done, b * HEADS + h)
                pool.tensor_tensor(dpart[0:CT, :, :], p[0:CT, 0:3, :], p[0:CT, 3:6, :], ALU.add).then_inc(dpart_done, 1)
                pool.tensor_tensor(dlat[0:LT, :], p[0:LT, 6, :], p[0:LT, 7, :], ALU.add).then_inc(dpart_done, 1)
                pool.wait_ge(dpart_done, n + 1)
                pool.tensor_tensor(dsum[0:CT, h % 4, :], dpart[0:CT, 0, :], dpart[0:CT, 1, :],
                                   ALU.add).then_inc(dpart_done, 1)
                pool.wait_ge(dpart_done, n + 3)
                pool.tensor_tensor(dsum[0:CT, h % 4, :], dsum[0:CT, h % 4, :], dpart[0:CT, 2, :],
                                   ALU.add).then_inc(dpart_done, 1)
                pool.wait_ge(dpart_done, n + 4)
                pool.tensor_tensor(dsum[0:LT, h % 4, :], dsum[0:LT, h % 4, :], dlat[0:LT, :],
                                   ALU.add).then_inc(dsum_done, 1)

            def inverse_root(ready, n, done, count):
                pool.wait_ge(ready, n)
                pool.tensor_tensor(rstd[:, 0:count], ve[:, 0:count], halfneg[:, 0:count], ALU.pow).then_inc(done, 1)

            def lo_tile(b, t):
                pool.wait_ge(xhi_done, b * TILES + (t + 1))
                cols = slice(AT[t], AT[t] + ROWS[t])
                pool.tensor_tensor(xT[:, 1, :, cols], xaff[:, t % 2, :, 0:ROWS[t]],
                                   xT[:, 0, :, cols].bitcast(F32), ALU.subtract).then_inc(xlo_done, 1)

            def batch(b, last):
                all_max(b, 0)
                all_max(b, 1)
                denominators(b, 0)
                all_max(b, 2)
                denominators(b, 1)
                all_max(b, 3)
                if not last:
                    inverse_root(ve_done, b * 3 + 4, rstd_done, 4)
                denominators(b, 2)
                denominators(b, 3)
                all_max(b, 4)
                all_max(b, 5)
                denominators(b, 4)
                if not last:
                    lo_tile(b + 1, 0)
                    lo_tile(b + 1, 1)
                denominators(b, 5)
                if not last:
                    lo_tile(b + 1, 2)
                    lo_tile(b + 1, 3)
                    inverse_root(ve_done, b * 3 + 5, rstd_done, 4)
                all_max(b, 6)
                if not last:
                    inverse_root(ve_done, b * 3 + 6, rstd_done, 2)
                all_max(b, 7)
                if not last:
                    lo_tile(b + 1, 4)
                    lo_tile(b + 1, 5)
                denominators(b, 6)
                if not last:
                    lo_tile(b + 1, 6)
                    lo_tile(b + 1, 7)
                denominators(b, 7)

            pool.memset(ident[:, :], 0.0).then_inc(ident_ready, 1)
            pool.memset(ident_b[:, :], 0.0).then_inc(ident_ready, 1)
            pool.wait_ge(ident_ready, 2)
            for m in (ident, ident_b):
                pool.affine_select(out=m[:, :], in_=m[:, :], compare_op=ALU.not_equal, fill=1.0, base=0,
                                   pattern=[[-1, P]], channel_multiplier=1).then_inc(ident_ready, 1)
            pool.wait_ge(const_ready, 3)
            inverse_root(ve_done, 1, rstd_done, 4)
            for t in range(4):
                lo_tile(0, t)
            inverse_root(ve_done, 2, rstd_done, 4)
            inverse_root(ve_done, 3, rstd_done, 2)
            for t in range(4, TILES):
                lo_tile(0, t)
            with pool.Fori(0, NA - 1) as b:
                batch(b, False)
            batch(NA - 1, True)

            def squares(g, j):
                pool.wait_ge(relu_done, g * FC + (j + 1))
                pool.wait_ge(h_lo, g * FC + max(j - 1, 0))
                pool.tensor_tensor(h32[:, j % 2, :], relu[:, j % 2, :], relu[:, j % 2, :],
                                   ALU.mult).then_inc(h_done, 1)

            def group(g, last):
                for j in range(FC):
                    squares(g, j)
                    if not last and j == FC - 2:
                        inverse_root(g_ve, g + 2, g_rstd, 4)

            inverse_root(g_ve, 1, g_rstd, 4)
            with pool.Fori(0, GROUPS - 1) as g:
                group(g, False)
            group(GROUPS - 1, True)


_ORDER = ["x", "ctx_1024", "g_xattn", "g_ffn", "L0_xattn_Wq", "L0_xattn_Wkv", "L0_xattn_Wout", "L0_xattn_gm",
          "L0_xattn_bm", "L0_xattn_gl", "L0_xattn_bl", "L0_ffn_W_fc", "L0_ffn_W_proj"]


def kernel(**inputs):
    import numpy as np
    import concourse.bacc as bacc
    from concourse import mybir as mb
    from concourse.bass_utils import run_bass_kernel_spmd

    def laid_out(name):
        a = np.asarray(inputs[name])
        if name in ("g_xattn", "g_ffn"):
            a = np.repeat(a.reshape(1, 1), 128, axis=0)
        elif a.ndim == 1:
            a = a.reshape(-1, 128).T
        elif name.startswith("L0_ffn"):
            a = a.T
        return np.ascontiguousarray(a)

    nc = bacc.Bacc("TRN2", target_bir_lowering=False, num_devices=1)
    arrays, args = {}, []
    for name in _ORDER:
        a = laid_out(name)
        arrays[f"in_{name}"] = a
        args.append(nc.dram_tensor(f"in_{name}", a.shape, mb.dt.from_np(a.dtype), kind="ExternalInput").ap())
    shape = np.asarray(inputs["x"]).shape
    args.append(nc.dram_tensor("out", shape, mb.dt.float32, kind="ExternalOutput").ap())
    flamingo_block(nc, *args)
    r = run_bass_kernel_spmd(nc, [arrays], core_ids=[0])
    return r.results[0]["out"]
```

```python
from contextlib import ExitStack

import concourse.bass as bass
from concourse import mybir

F32 = mybir.dt.float32
F32R = mybir.dt.float32r
BF16 = mybir.dt.bfloat16
ALU = mybir.AluOpType
ACT = mybir.ActivationFunctionType
AX = mybir.AxisListType
RMAX = bass.bass_isa.ReduceOp.max

P = 128
EPS = 1e-5
LOWEST = -3.0e38
BETA = 0.9
THRESHOLD = 1.0
STEPS = 5


def flamingo_block(nc, x, ctx_in, g_xattn, g_ffn, Wq, Wkv, Wout, gm, bm, gl, bl, WfcT, WprojT, out):
    B, L, D = x.shape
    T = ctx_in.shape[1]
    F = WfcT.shape[1]
    DH = 64
    HEADS = D // DH
    DC = D // P
    LT = L // 2
    CTX_TILES = 6
    CT = T // CTX_TILES
    TILES = CTX_TILES + 2
    KEYS = T + L
    HALF = (KEYS // 2 + 1) // 2 * 2
    PAIRS = HEADS // 2
    QSCALE = float(DH) ** 0.5
    ROWS = [CT] * CTX_TILES + [LT] * 2
    AT = [t * CT for t in range(CTX_TILES)] + [T, T + LT]
    BANKS = TILES // 2
    PASSES = ((0, 0), (0, 1), (1, 0))
    TG = 2 * L
    GROUPS = B // 2
    FC = F // P
    assert CT * CTX_TILES == T and CT <= P and HALF <= 512 and D == 512

    x_flat = x.rearrange("b l d -> (b l) d")
    out_flat = out.rearrange("b l d -> (b l) d")
    x1_dram = nc.dram_tensor("x1_scratch", (B * L, D), F32, kind="Internal").ap()

    keep = ExitStack()
    with keep:
        def sb(stack, name, shape, dt=F32):
            return stack.enter_context(nc.sbuf_tensor(name, shape, dt))

        def sem(name):
            return keep.enter_context(nc.semaphore(name))

        ident = sb(keep, "ident", [P, P])
        ident_b = sb(keep, "ident_b", [P, P], BF16)
        ones = sb(keep, "ones", [P, DH])
        gate_in = sb(keep, "gate_in", [P, 2])
        gate = sb(keep, "gate", [P, 2])
        halfneg = sb(keep, "halfneg", [P, 10])
        bn = sb(keep, "bn", [P, 10, 6])
        mv = sb(keep, "mv", [P, 10, 2])
        ve = sb(keep, "ve", [P, 10])
        rstd = sb(keep, "rstd", [P, 10])
        tick = sb(keep, "tick", [P, 3])

        score = keep.enter_context(nc.psum_tensor("score", [P, BANKS, 512], F32))
        work = [keep.enter_context(nc.psum_tensor(f"work{i}", [P, 512], F32)) for i in range(3)]
        heads_out = keep.enter_context(nc.psum_tensor("heads_out", [P, 512], F32))

        a = ExitStack()
        wq = sb(a, "wq", [P, 2, DC, D], F32R)
        wk = sb(a, "wk", [P, 2, DC, D], F32R)
        wv = sb(a, "wv", [P, 2, DC, D], F32R)
        xT = sb(a, "xT", [P, 2, DC, KEYS], F32R)
        xin = sb(a, "xin", [P, TILES, D])
        affine = sb(a, "affine", [P, 4, D])
        kst = sb(a, "kst", [P, 2, 2, KEYS], F32R)
        qst = sb(a, "qst", [P, 2, 2, 2, L], F32R)
        vals = sb(a, "vals", [P, TILES, D])
        probs = sb(a, "probs", [P, 4, TILES * L])
        mx = sb(a, "mx", [P, 2, L])
        mxb = sb(a, "mxb", [P, 2, L])
        dsum = sb(a, "dsum", [P, 4, L])
        on32 = sb(a, "on32", [P, L])
        oT = sb(a, "oT", [P, 2, PAIRS, L], F32R)
        wo = sb(a, "wo", [P, 2, DC, D], F32R)
        xres = sb(a, "xres", [P, 2, D])
        a.close()

        bb = ExitStack()
        wf = sb(bb, "wf", [P, 2, FC, DC * P], F32R)
        neuron = sb(bb, "neuron", [P, 4096])
        zt = sb(bb, "zt", [P, 4, D])
        zT = sb(bb, "zT", [P, 2, DC, TG], F32R)
        wp = sb(bb, "wp", [P, 2, FC, D], F32R)
        fin = sb(bb, "fin", [P, 4, D])
        relu = sb(bb, "relu", [P, 2, TG])
        h32 = sb(bb, "h32", [P, 2, TG])
        hT = sb(bb, "hT", [P, 3, 2, TG], F32R)
        spikes = sb(bb, "spikes", [P, DC * TG], BF16)
        bb.close()

        EARLY = 6
        SLOTS = 8
        PIECES = [("up", j) for j in range(EARLY)]
        for j in range(FC):
            PIECES.append(("down", j))
            if j + EARLY < FC:
                PIECES.append(("up", j + EARLY))

        AT_START = range(EARLY, EARLY + 4)
        WITH = [range(EARLY + 4 + 2 * j, min(EARLY + 6 + 2 * j, len(PIECES))) for j in range(FC)]
        assert sum(map(len, WITH)) + EARLY + 4 == len(PIECES)

        def stage(n):
            return neuron[:, n % SLOTS * 512:(n % SLOTS + 1) * 512]

        def piece(n, part):
            kind, j = PIECES[n]
            return (wf if kind == "up" else wp)[:, part, j, :]

        ident_ready = sem("ident_ready")
        const_ready = sem("const_ready")
        small_in = sem("small_in")
        affine_in = sem("affine_in")
        gate_ready = sem("gate_ready")
        gate_half = sem("gate_half")
        w_in = [sem(f"w_in{i}") for i in range(4)]
        w_hi = sem("w_hi")
        w_lo = sem("w_lo")
        pad_ready = sem("pad_ready")
        x_in = [sem(f"x_in{i}") for i in range(TILES)]
        bn_done = sem("bn_done")
        mv_done = sem("mv_done")
        ve_done = sem("ve_done")
        rstd_done = sem("rstd_done")
        ln_half = sem("ln_half")
        centred = sem("centred")
        gain_done = sem("gain_done")
        ln_done = sem("ln_done")
        tr_done = sem("tr_done")
        xhi_done = sem("xhi_done")
        xlo_done = sem("xlo_done")
        kq_mm = sem("kq_mm")
        kq_hi = sem("kq_hi")
        kq_done = sem("kq_done")
        v_mm = sem("v_mm")
        v_done = sem("v_done")
        s_mm = sem("s_mm")
        s_copied = sem("s_copied")
        max_done = sem("max_done")
        maxb_done = sem("maxb_done")
        sub_done = sem("sub_done")
        exp_done = sem("exp_done")
        dchain = sem("dchain")
        dsum_done = sem("dsum_done")
        pv_done = sem("pv_done")
        rden_done = sem("rden_done")
        on_done = sem("on_done")
        ohi_done = sem("ohi_done")
        o_done = sem("o_done")
        wo_mm = sem("wo_mm")
        x1_done = sem("x1_done")
        res_in = [sem(f"res_in{i}") for i in range(2)]
        x1_out = [sem(f"x1_out{i}") for i in range(2)]
        fw_in = [sem(f"fw_in{i}") for i in range(SLOTS)]
        fw_hi = sem("fw_hi")
        fw_lo = sem("fw_lo")
        zt_in = sem("zt_in")
        fin_in = sem("fin_in")
        g_bn = sem("g_bn")
        g_mv = sem("g_mv")
        g_ve = sem("g_ve")
        g_rstd = sem("g_rstd")
        z_done = sem("z_done")
        zt_mm = sem("zt_mm")
        z_hi = sem("z_hi")
        z_lo = sem("z_lo")
        up_mm = sem("up_mm")
        relu_done = sem("relu_done")
        h_done = sem("h_done")
        h_hi = sem("h_hi")
        h_lo = sem("h_lo")
        down_mm = sem("down_mm")
        y_mm = sem("y_mm")
        y_done = sem("y_done")
        lif = sem("lif")
        spk_done = sem("spk_done")
        spkT_mm = sem("spkT_mm")
        fin_done = sem("fin_done")
        fin_out = sem("fin_out")

        block = keep.enter_context(nc.Block())

        def tile_src(b, t):
            if t < CTX_TILES:
                return ctx_in[b, AT[t]:AT[t] + CT, :]
            return x[b, (t - CTX_TILES) * LT:(t - CTX_TILES + 1) * LT, :]

        NA = B
        probs_flat = probs[:, :, :].rearrange("p h c -> p (h c)")
        staged = [vals[:, 0:DC, :], vals[:, DC:2 * DC, :]] + [
            probs_flat[:, TILES * L + 2048 * i:TILES * L + 2048 * (i + 1)].rearrange("p (k n) -> p k n", k=DC)
            for i in range(2)]
        LIF_OPS = 24

        @block.sync
        def _(sp):
            def load_tile(b, t):
                sp.dma_start(xin[0:ROWS[t], t, :], tile_src(b, t)).then_inc(x_in[t], 16)

            def load_residual(b, i):
                sp.dma_start(xres[0:LT, i, :], x[b, i * LT:(i + 1) * LT, :]).then_inc(res_in[i], 16)

            def refill(b):
                for t in range(TILES):
                    sp.wait_ge(tr_done, b * TILES + (t + 1))
                    load_tile(b + 1, t)

            def residual(b, last):
                for i in range(2):
                    sp.wait_ge(x1_done, b * 2 + (i + 1))
                    rows = x1_dram.rearrange("(b i r) d -> b i r d", b=B, i=2)[b, i]
                    sp.dma_start(rows, xres[0:LT, i, :]).then_inc(x1_out[i], 16)
                    sp.wait_ge(x1_out[i], b * 16 + 16)
                    if not last:
                        load_residual(b + 1, i)

            def load_weight(i, w, at):
                sp.dma_start(at, w.rearrange("(k p) n -> p k n", p=P)).then_inc(w_in[i], 16)

            for t in range(4):
                load_tile(0, t)
            for i, v in enumerate((gm, bm)):
                sp.dma_start(affine[:, i, :], v.partition_broadcast(P)).then_inc(affine_in, 16)
            load_weight(0, Wkv[:, 0:D], staged[0])
            for t in range(4, TILES):
                load_tile(0, t)
            for i, v in enumerate((gl, bl)):
                sp.dma_start(affine[:, 2 + i, :], v.partition_broadcast(P)).then_inc(affine_in, 16)
            load_weight(1, Wq, staged[1])
            load_weight(2, Wkv[:, D:2 * D], staged[2])
            load_weight(3, Wout, staged[3])
            sp.dma_start(gate_in[:, 0:1], g_xattn).then_inc(small_in, 16)
            sp.dma_start(gate_in[:, 1:2], g_ffn).then_inc(small_in, 16)
            for i in range(2):
                load_residual(0, i)
            refill(0)
            with sp.Fori(1, NA - 1) as b:
                refill(b)
                residual(b - 1, False)
            residual(NA - 2, False)

            def group_rows(d, g):
                return d.rearrange("(g i r) d -> g r i d", g=GROUPS, i=4)[g]

            def load_z(g):
                sp.dma_start(zt[0:LT, :, :], group_rows(x1_dram, g)).then_inc(zt_in, 16)

            def load_fin(g):
                sp.dma_start(fin[0:LT, :, :], group_rows(x1_dram, g)).then_inc(fin_in, 16)

            def store_fin(g):
                for i in range(4):
                    sp.wait_ge(fin_done, g * 4 + (i + 1))
                    rows = out_flat.rearrange("(g i r) d -> g i r d", g=GROUPS, i=4)[g, i]
                    sp.dma_start(rows, fin[0:LT, i, :]).then_inc(fin_out, 16)
                sp.wait_ge(fin_out, g * 64 + 64)

            def group(g, last):
                if not last:
                    sp.wait_ge(zt_mm, g * 4 + 4)
                    load_z(g + 1)
                store_fin(g - 1)
                load_fin(g)

            def load_piece(n):
                kind, j = PIECES[n]
                if n >= SLOTS:
                    sp.wait_ge(fw_lo, n - SLOTS + 1)
                if kind == "up":
                    sp.dma_start(stage(n).rearrange("p (k f) -> p k f", k=DC),
                                 WfcT.rearrange("(k p) (j f) -> j p k f", p=P, f=P)[j]).then_inc(fw_in[n % SLOTS], 16)
                else:
                    sp.dma_start(stage(n), WprojT[j * P:(j + 1) * P, :]).then_inc(fw_in[n % SLOTS], 16)

            sp.wait_ge(kq_mm, NA * 12)
            sp.wait_ge(v_mm, NA * TILES)
            load_z(0)
            for n in range(EARLY):
                load_piece(n)
            residual(NA - 1, True)
            for n in range(EARLY, len(PIECES)):
                load_piece(n)
            load_fin(0)
            sp.wait_ge(zt_mm, 4)
            load_z(1)
            with sp.Fori(1, GROUPS - 1) as g:
                group(g, False)
            group(GROUPS - 1, True)
            store_fin(GROUPS - 1)

        @block.tensor
        def _(pe):
            def product(bank, lhs, rhs, chunks, passes=PASSES):
                n = 0
                for i, j in passes:
                    for k in range(chunks):
                        mm = pe.matmul(bank, lhs(i, k), rhs(j, k), start=(n == 0),
                                       stop=(n == len(passes) * chunks - 1))
                        n += 1
                return mm

            def transposes(b, t, first):
                if t < 3:
                    if not first:
                        pe.wait_ge(kq_done, b * 12 - 2 + t)
                else:
                    pe.wait_ge(xlo_done, b * TILES + (t - 2))
                pe.wait_ge(ln_done, b * TILES + (t + 1))
                bank = work[(t + 2) % 3]
                for k in range(DC):
                    mm = pe.transpose(bank[:, k * P:k * P + ROWS[t]], xin[0:ROWS[t], t, k * P:(k + 1) * P],
                                      ident[0:ROWS[t], 0:ROWS[t]])
                mm.then_inc(tr_done, 1)

            def keys_queries(b, c):
                cols = slice(c * P, (c + 1) * P)
                for u in range(3):
                    if c == 0:
                        if u == 0:
                            pe.wait_ge(xlo_done, b * TILES + TILES)
                    elif c == 1:
                        pe.wait_ge(kq_done, b * 12 + 3)
                        if u > 0:
                            pe.wait_ge(x1_done, b * 2)
                    elif c == 2:
                        pe.wait_ge(v_done, b * TILES + (6 + u))
                    else:
                        pe.wait_ge(kq_done, b * 12 + (7 + u))
                    bank = work[((25, 0, 11, 14)[c] + u) % 3]
                    if u < 2:
                        lo, hi = (0, HALF) if u == 0 else (HALF, KEYS)
                        mm = product(bank[:, 0:hi - lo], lambda i, k: wk[:, i, k, cols],
                                     lambda i, k: xT[:, i, k, lo:hi], DC)
                    else:
                        mm = product(bank[:, 0:L], lambda i, k: wq[:, i, k, cols],
                                     lambda i, k: xT[:, i, k, T:KEYS], DC)
                    mm.then_inc(kq_mm, 1)

            def values(b, t):
                if t < 3:
                    pe.wait_ge(kq_done, b * 12 + (4 + t))
                else:
                    pe.wait_ge(v_done, b * TILES + (t - 2))
                product(work[t % 3][0:ROWS[t], :], lambda i, k: xT[:, i, k, AT[t]:AT[t] + ROWS[t]],
                        lambda i, k: wv[:, i, k, :], DC).then_inc(v_mm, 1)

            def scores(b, h):
                s, e = h // 2 % 2, h % 2
                pe.wait_ge(kq_done, b * 12 + (3 * (h // 2) + 3))
                for t in range(TILES):
                    if t % 2 == 0:
                        pe.wait_ge(s_copied, (b * HEADS + h) * BANKS - (BANKS - 1 - t // 2 if h else 0))
                    for j in range(2):
                        mm = pe.matmul(score[0:ROWS[t], t // 2, t % 2 * L:(t % 2 + 1) * L],
                                       kst[:, s, e, AT[t]:AT[t] + ROWS[t]], qst[:, s, j, e, :],
                                       start=(j == 0), stop=(j == 1))
                    if t % 2:
                        mm.then_inc(s_mm, 1)

            def attend(b, p):
                pe.wait_ge(v_done, b * TILES + TILES)
                pe.wait_ge(o_done, b * PAIRS + p)
                pe.wait_ge(exp_done, b * HEADS + (2 * p + 2))
                for t in range(TILES):
                    for e in range(2):
                        h = 2 * p + e
                        pe.matmul(heads_out[e * DH:(e + 1) * DH, 0:L], vals[0:ROWS[t], t, h * DH:(h + 1) * DH],
                                  probs[0:ROWS[t], h % 4, t * L:(t + 1) * L],
                                  start=(t == 0), stop=(t == TILES - 1))
                pe.wait_ge(dsum_done, b * HEADS + (2 * p + 2))
                for e in range(2):
                    mm = pe.matmul(heads_out[e * DH:(e + 1) * DH, L:2 * L], ones[0:CT, :],
                                   dsum[0:CT, (2 * p + e) % 4, :], start=True, stop=True)
                mm.then_inc(pv_done, 1)

            def out_projection(b, last):
                for pairs in (range(PAIRS - 1), range(PAIRS - 1, PAIRS)):
                    pe.wait_ge(o_done, b * PAIRS + pairs[-1] + 1)
                    for i in range(2):
                        if pairs[0] == 0:
                            pe.wait_ge(kq_done, b * 12 + (12 if last else 13 + i))
                        for p in pairs:
                            for n, (m, k) in enumerate(PASSES):
                                mm = pe.matmul(work[(28 + i) % 3][0:LT, :], oT[:, m, p, i * LT:(i + 1) * LT],
                                               wo[:, k, p, :], start=(p == 0 and n == 0),
                                               stop=(p == PAIRS - 1 and n == 2))
                        if pairs[0]:
                            mm.then_inc(wo_mm, 1)

            def batch(b, last):
                def ahead(*ts):
                    if not last:
                        for t in ts:
                            transposes(b + 1, t, False)

                scores(b, 0)
                scores(b, 1)
                keys_queries(b, 1)
                pe.wait_ge(w_lo, 4)
                values(b, 0)
                scores(b, 2)
                scores(b, 3)
                for t in range(1, TILES):
                    values(b, t)
                keys_queries(b, 2)
                attend(b, 0)
                scores(b, 4)
                scores(b, 5)
                keys_queries(b, 3)
                ahead(0, 1)
                attend(b, 1)
                ahead(2, 3)
                scores(b, 6)
                ahead(4, 5)
                scores(b, 7)
                ahead(6, 7)
                attend(b, 2)
                if not last:
                    keys_queries(b + 1, 0)
                attend(b, 3)
                out_projection(b, last)

            pe.wait_ge(ident_ready, 4)
            pe.wait_ge(const_ready, 1)
            for t in range(TILES):
                transposes(0, t, True)
            pe.wait_ge(w_lo, 2)
            keys_queries(0, 0)
            with pe.Fori(0, NA - 1) as b:
                batch(b, False)
            batch(NA - 1, True)

            def group_transposes(g, first):
                for i in range(4):
                    pe.wait_ge(z_done, g * 4 + (i + 1))
                    if i >= 2:
                        pe.wait_ge(z_lo, g * 4 + (i - 1))
                    elif not first:
                        pe.wait_ge(fin_done, g * 4 - 4)
                    bank = (work[2], heads_out)[i % 2]
                    for k in range(DC):
                        mm = pe.transpose(bank[:, k * LT:(k + 1) * LT], zt[0:LT, i, k * P:(k + 1) * P],
                                          ident[0:LT, 0:LT])
                    mm.then_inc(zt_mm, 1)

            def up(g, j):
                if j < 2:
                    pe.wait_ge(relu_done, g * FC)
                else:
                    pe.wait_ge(relu_done, g * FC + (j - 1))
                pe.wait_ge(fw_lo, PIECES.index(("up", j)) + 1)
                product(work[j % 2][:, 0:TG], lambda i, k: wf[:, i, j, k * P:(k + 1) * P],
                        lambda i, k: zT[:, i, k, :], DC).then_inc(up_mm, 1)

            def down(g, j):
                pe.wait_ge(h_lo, g * FC + (j + 1))
                if j == 0:
                    pe.wait_ge(y_done, g * DC)
                pe.wait_ge(fw_lo, PIECES.index(("down", j)) + 1)
                for d in range(DC):
                    for n, (w, a_) in enumerate(PASSES):
                        mm = pe.matmul(score[:, d, 0:TG], wp[:, w, j, d * P:(d + 1) * P], hT[:, j % 3, a_, :],
                                       start=(j == 0 and n == 0), stop=(j == FC - 1 and n == 2))
                    if j == FC - 1:
                        mm.then_inc(y_mm, 1)
                    elif d == DC - 1:
                        mm.then_inc(down_mm, 1)

            def spikes_back(g, tiles):
                pe.wait_ge(spk_done, g * 2 + 2)
                for i in tiles:
                    if i >= 2:
                        pe.wait_ge(fin_done, g * 4 + (i - 1))
                    bank = (work[2], heads_out)[i % 2][:, 0:D // 2].bitcast(BF16)
                    for k in range(DC):
                        mm = pe.transpose(bank[0:LT, k * P:(k + 1) * P],
                                          spikes[:, k * TG + i * LT:k * TG + (i + 1) * LT], ident_b[:, :])
                    mm.then_inc(spkT_mm, 1)

            def group(g, first, last):
                pe.wait_ge(z_lo, g * 4 + 4)
                for j in range(FC):
                    up(g, j)
                    if j >= 2:
                        down(g, j - 2)
                    if not first and j in (13, 14):
                        spikes_back(g - 1, (0, 1) if j == 13 else (2, 3))
                if not last:
                    group_transposes(g + 1, first)
                down(g, FC - 2)
                down(g, FC - 1)

            pe.wait_ge(x1_done, NA * 2)
            group_transposes(0, True)
            group(0, True, False)
            with pe.Fori(1, GROUPS - 1) as g:
                group(g, False, False)
            group(GROUPS - 1, False, True)
            spikes_back(GROUPS - 1, range(4))

        @block.scalar
        def _(act):
            def copy_scores(b, h):
                act.wait_ge(pv_done, b * PAIRS + max(h // 2 - 1, 0))
                for k in range(BANKS):
                    act.wait_ge(s_mm, (b * HEADS + h) * BANKS + (k + 1))
                    r = ROWS[2 * k]
                    act.activation(probs[0:r, h % 4, 2 * k * L:(2 * k + 2) * L], score[0:r, k, 0:2 * L],
                                   ACT.Copy).then_inc(s_copied, 1)

            def exponentials(b, h):
                act.wait_ge(sub_done, (b * HEADS + h) * 2 + 2)
                act.activation(probs[0:CT, h % 4, 0:CTX_TILES * L], probs[0:CT, h % 4, 0:CTX_TILES * L], ACT.Exp)
                act.activation(probs[0:LT, h % 4, CTX_TILES * L:], probs[0:LT, h % 4, CTX_TILES * L:],
                               ACT.Exp).then_inc(exp_done, 1)

            def kq_hi_parts(b, c):
                s = c % 2
                if c == 1:
                    act.wait_ge(s_mm, b * HEADS * BANKS)
                elif c >= 2:
                    act.wait_ge(s_mm, b * HEADS * BANKS + (2 * c - 2) * BANKS)
                for u in range(3):
                    act.wait_ge(kq_mm, b * 12 + (3 * c + u + 1))
                    bank = work[((25, 0, 11, 14)[c] + u) % 3]
                    for e in range(2):
                        rows = slice(e * DH, (e + 1) * DH)
                        if u < 2:
                            lo, hi = (0, HALF) if u == 0 else (HALF, KEYS)
                            act.activation(kst[rows, s, e, lo:hi], bank[rows, 0:hi - lo],
                                           ACT.Copy).then_inc(kq_hi, 1)
                        else:
                            act.activation(qst[0:DH, s, 0, e, :], bank[rows, 0:L], ACT.Copy, scale=QSCALE)
                            act.activation(qst[DH:P, s, 0, e, :], bank[rows, 0:L], ACT.Copy,
                                           scale=QSCALE).then_inc(kq_hi, 1)

            def copy_values(b, *ts):
                act.wait_ge(pv_done, b * PAIRS)
                for t in ts:
                    act.wait_ge(v_mm, b * TILES + (t + 1))
                    act.activation(vals[0:ROWS[t], t, :], work[t % 3][0:ROWS[t], :], ACT.Copy).then_inc(v_done, 1)

            def hi_tile(b, t):
                if t == 0:
                    act.wait_ge(kq_mm, b * 12)
                act.wait_ge(tr_done, b * TILES + (t + 1))
                act.activation(xT[:, 0, :, AT[t]:AT[t] + ROWS[t]],
                               work[(t + 2) % 3][:, :].rearrange("p (k r) -> p k r", k=DC)[:, :, 0:ROWS[t]],
                               ACT.Copy).then_inc(xhi_done, 1)

            def batch(b, last):
                def ahead(*ts):
                    if not last:
                        for t in ts:
                            hi_tile(b + 1, t)

                copy_scores(b, 0)
                copy_scores(b, 1)
                kq_hi_parts(b, 1)
                exponentials(b, 0)
                copy_values(b, 0)
                copy_scores(b, 2)
                exponentials(b, 1)
                copy_scores(b, 3)
                copy_values(b, 1, 2)
                exponentials(b, 2)
                copy_values(b, 3, 4)
                exponentials(b, 3)
                copy_values(b, 5, 6, 7)
                kq_hi_parts(b, 2)
                copy_scores(b, 4)
                copy_scores(b, 5)
                kq_hi_parts(b, 3)
                ahead(0, 1)
                exponentials(b, 4)
                ahead(2, 3)
                exponentials(b, 5)
                copy_scores(b, 6)
                ahead(4, 5)
                copy_scores(b, 7)
                ahead(6, 7)
                exponentials(b, 6)
                exponentials(b, 7)
                if not last:
                    kq_hi_parts(b + 1, 0)

            for i, w in enumerate((wk, wq, wv, wo)):
                act.wait_ge(w_in[i], 16)
                act.activation(w[:, 0], staged[i], ACT.Copy).then_inc(w_hi, 1)
                if i == 1:
                    for t in range(TILES):
                        hi_tile(0, t)
                    kq_hi_parts(0, 0)
            act.wait_ge(small_in, 32)
            act.activation(gate[:, :], gate_in[:, :], ACT.Tanh).then_inc(gate_half, 1)
            act.wait_ge(w_lo, 4)
            act.wait_ge(pad_ready, 2)
            with act.Fori(0, NA - 1) as b:
                batch(b, False)
            batch(NA - 1, True)

            def split_weights(*pieces):
                for n in pieces:
                    act.wait_ge(fw_in[n % SLOTS], 16 * (n // SLOTS + 1))
                    act.activation(piece(n, 0), stage(n), ACT.Copy).then_inc(fw_hi, 1)

            def group_hi(g):
                for i in range(4):
                    act.wait_ge(zt_mm, g * 4 + (i + 1))
                    act.activation(zT[:, 0, :, i * LT:(i + 1) * LT],
                                   (work[2], heads_out)[i % 2][:, 0:TG].rearrange("p (k r) -> p k r", k=DC),
                                   ACT.Copy).then_inc(z_hi, 1)

            def group(g, first, last):
                for j in range(FC):
                    act.wait_ge(up_mm, g * FC + (j + 1))
                    if j < 2:
                        act.wait_ge(h_done, g * FC)
                    else:
                        act.wait_ge(h_done, g * FC + (j - 1))
                    act.activation(relu[:, j % 2, :], work[j % 2][:, 0:TG], ACT.Relu).then_inc(relu_done, 1)
                    act.wait_ge(h_done, g * FC + (j + 1))
                    if j < 3:
                        act.wait_ge(y_mm, g * DC)
                    else:
                        act.wait_ge(down_mm, g * (FC - 1) + (j - 2))
                    act.activation(hT[:, j % 3, 0, :], h32[:, j % 2, :], ACT.Copy).then_inc(h_hi, 1)
                    if first:
                        split_weights(*WITH[j])
                if not last:
                    group_hi(g + 1)
                act.wait_ge(spk_done, g * 2)
                act.wait_ge(fw_lo, len(PIECES))
                for d in range(DC):
                    act.wait_ge(y_mm, g * DC + (d + 1))
                    act.activation(neuron[:, d * TG:(d + 1) * TG], score[:, d, 0:TG], ACT.Copy).then_inc(y_done, 1)

            split_weights(*range(EARLY))
            group_hi(0)
            split_weights(*AT_START)
            group(0, True, False)
            with act.Fori(1, GROUPS - 1) as g:
                group(g, False, False)
            group(GROUPS - 1, False, True)

        @block.vector
        def _(dve):
            def scale_max(b, h):
                dve.wait_ge(s_copied, (b * HEADS + h + 1) * BANKS)
                dve.wait_ge(maxb_done, b * HEADS + max(h - 1, 0))
                dve.tensor_reduce(mx[0:CT, h % 2, :],
                                  probs[0:CT, h % 4, :].rearrange("p (t l) -> p l t", t=TILES),
                                  AX.X, ALU.max).then_inc(max_done, 1)

            def subtract(b, h):
                dve.wait_ge(maxb_done, b * HEADS + (h + 1))
                for r, lo, n in ((CT, 0, CTX_TILES), (LT, CTX_TILES, 2)):
                    v = probs[0:r, h % 4, lo * L:(lo + n) * L].rearrange("p (t l) -> p t l", t=n)
                    dve.tensor_tensor(v, v, mxb[0:r, h % 2:h % 2 + 1, :].to_broadcast([r, n, L]),
                                      ALU.subtract).then_inc(sub_done, 1)

            def kq_lo_parts(b, c):
                s = c % 2
                for u in range(3):
                    bank = work[((25, 0, 11, 14)[c] + u) % 3]
                    for e in range(2):
                        rows = slice(e * DH, (e + 1) * DH)
                        other = slice((1 - e) * DH, (2 - e) * DH)
                        dve.wait_ge(kq_hi, (b * 12 + (3 * c + u)) * 2 + (e + 1))
                        if u < 2:
                            lo, hi = (0, HALF) if u == 0 else (HALF, KEYS)
                            ins = dve.tensor_tensor(kst[other, s, e, lo:hi], bank[rows, 0:hi - lo],
                                                    kst[rows, s, e, lo:hi].bitcast(F32), ALU.subtract)
                        else:
                            for r in (slice(0, DH), slice(DH, P)):
                                ins = dve.scalar_tensor_tensor(qst[r, s, 1, e, :], bank[rows, 0:L], QSCALE,
                                                               qst[rows, s, 0, e, :].bitcast(F32),
                                                               ALU.mult, ALU.subtract)
                    ins.then_inc(kq_done, 1)

            def normalise(b, p):
                dve.wait_ge(pv_done, b * PAIRS + (p + 1))
                n = b * PAIRS + p
                dve.reciprocal(on32[:, :], heads_out[:, L:2 * L]).then_inc(rden_done, 1)
                dve.wait_ge(rden_done, n + 1)
                dve.tensor_tensor(on32[:, :], heads_out[:, 0:L], on32[:, :], ALU.mult).then_inc(on_done, 1)
                dve.wait_ge(on_done, n + 1)
                dve.wait_ge(wo_mm, b * 2)
                dve.tensor_copy(oT[:, 0, p, :], on32[:, :]).then_inc(ohi_done, 1)
                dve.wait_ge(ohi_done, n + 1)
                dve.tensor_tensor(oT[:, 1, p, :], on32[:, :], oT[:, 0, p, :].bitcast(F32),
                                  ALU.subtract).then_inc(o_done, 1)

            GOES = ([0, 1, 2, 3], [4, 5, 6, 7], [6, 7])

            def statistics(b, go):
                first, n = go * 4, len(GOES[go])
                for i, t in enumerate(GOES[go]):
                    if go < 2:
                        dve.wait_ge(x_in[t], b * 16 + 16)
                    else:
                        dve.wait_ge(ln_half, b * 2 + (i + 1))
                    dve.bn_stats(bn[0:ROWS[t], first + i, :], xin[0:ROWS[t], t, :]).then_inc(bn_done, 1)
                dve.wait_ge(bn_done, b * 10 + (first + n))
                dve.tensor_copy(tick[:, 0:1], halfneg[:, 0:1])
                for i, t in enumerate(GOES[go]):
                    dve.bn_aggr(mv[0:ROWS[t], first + i, :], bn[0:ROWS[t], first + i, :]).then_inc(mv_done, 1)
                dve.wait_ge(mv_done, b * 10 + (first + n))
                dve.tensor_scalar(ve[:, first:first + n], mv[:, first:first + n, 1], EPS, None,
                                  ALU.add).then_inc(ve_done, 1)

            def centre(b, go, *ts):
                dve.wait_ge(rstd_done, b * 3 + (go + 1))
                for t in ts:
                    r, i = ROWS[t], go * 4 + GOES[go].index(t)
                    dve.tensor_scalar(xin[0:r, t, :], xin[0:r, t, :], mv[0:r, i, 0:1], rstd[0:r, i:i + 1],
                                      ALU.subtract, ALU.mult
                                      ).then_inc(ln_half if go == 1 and t >= CTX_TILES else centred, 1)

            def lo_tile(b, t):
                dve.wait_ge(xhi_done, b * TILES + (t + 1))
                cols = slice(AT[t], AT[t] + ROWS[t])
                dve.tensor_tensor(xT[:, 1, :, cols],
                                  work[(t + 2) % 3][:, :].rearrange("p (k r) -> p k r", k=DC)[:, :, 0:ROWS[t]],
                                  xT[:, 0, :, cols].bitcast(F32), ALU.subtract).then_inc(xlo_done, 1)

            def gated_residual(b):
                for i in range(2):
                    dve.wait_ge(wo_mm, b * 2 + (i + 1))
                    dve.wait_ge(res_in[i], b * 16 + 16)
                    dve.scalar_tensor_tensor(xres[0:LT, i, :], work[(28 + i) % 3][0:LT, :], gate[0:LT, 0:1],
                                             xres[0:LT, i, :], ALU.mult, ALU.add).then_inc(x1_done, 1)

            def group_statistics(g):
                dve.wait_ge(zt_in, g * 16 + 16)
                for i in range(4):
                    dve.bn_stats(bn[0:LT, i, :], zt[0:LT, i, :]).then_inc(g_bn, 1)
                dve.wait_ge(g_bn, g * 4 + 4)
                dve.tensor_copy(tick[:, 0:1], halfneg[:, 0:1])
                for i in range(4):
                    dve.bn_aggr(mv[0:LT, i, :], bn[0:LT, i, :]).then_inc(g_mv, 1)
                dve.wait_ge(g_mv, g * 4 + 4)
                dve.tensor_scalar(ve[:, 0:4], mv[:, 0:4, 1], EPS, None, ALU.add).then_inc(g_ve, 1)

            def group_centre(g):
                dve.wait_ge(g_rstd, g + 1)
                for i in range(4):
                    dve.tensor_scalar(zt[0:LT, i, :], zt[0:LT, i, :], mv[0:LT, i, 0:1], rstd[0:LT, i:i + 1],
                                      ALU.subtract, ALU.mult).then_inc(z_done, 1)

            def split_weights(*pieces):
                for n in pieces:
                    dve.wait_ge(fw_hi, n + 1)
                    dve.tensor_tensor(piece(n, 1), stage(n), piece(n, 0).bitcast(F32),
                                      ALU.subtract).then_inc(fw_lo, 1)

            def batch(b, last):
                def ahead(*ts):
                    if not last:
                        for t in ts:
                            lo_tile(b + 1, t)

                scale_max(b, 0)
                scale_max(b, 1)
                subtract(b, 0)
                kq_lo_parts(b, 1)
                subtract(b, 1)
                scale_max(b, 2)
                scale_max(b, 3)
                subtract(b, 2)
                if not last:
                    statistics(b + 1, 0)
                    statistics(b + 1, 1)
                subtract(b, 3)
                if not last:
                    centre(b + 1, 0, 0, 1, 2, 3)
                    centre(b + 1, 1, 4, 5, 6, 7)
                    statistics(b + 1, 2)
                    centre(b + 1, 2, 6, 7)
                kq_lo_parts(b, 2)
                normalise(b, 0)
                scale_max(b, 4)
                scale_max(b, 5)
                subtract(b, 4)
                kq_lo_parts(b, 3)
                ahead(0, 1)
                subtract(b, 5)
                normalise(b, 1)
                ahead(2, 3)
                scale_max(b, 6)
                ahead(4, 5)
                scale_max(b, 7)
                subtract(b, 6)
                ahead(6, 7)
                subtract(b, 7)
                if last:
                    group_statistics(0)
                normalise(b, 2)
                if not last:
                    kq_lo_parts(b + 1, 0)
                else:
                    group_centre(0)
                    split_weights(*range(EARLY))
                normalise(b, 3)
                gated_residual(b)

            def split_lo(i, w):
                dve.wait_ge(w_hi, i + 1)
                dve.tensor_tensor(w[:, 1], staged[i], w[:, 0].bitcast(F32), ALU.subtract).then_inc(w_lo, 1)

            dve.memset(ones[:, :], 1.0).then_inc(const_ready, 1)
            dve.memset(halfneg[:, :], -0.5).then_inc(const_ready, 1)
            dve.memset(mv[:, :, :], 1.0).then_inc(const_ready, 1)
            dve.memset(mx[:, :, :], LOWEST).then_inc(pad_ready, 1)
            dve.wait_ge(const_ready, 3)
            statistics(0, 0)
            centre(0, 0, 0, 1, 2, 3)
            split_lo(0, wk)
            statistics(0, 1)
            centre(0, 1, 4, 5, 6, 7)
            statistics(0, 2)
            centre(0, 2, 6, 7)
            split_lo(1, wq)
            for t in range(TILES):
                lo_tile(0, t)
            kq_lo_parts(0, 0)
            split_lo(2, wv)
            split_lo(3, wo)
            dve.wait_ge(w_lo, 4)
            dve.memset(probs[64:P, :, CTX_TILES * L:], LOWEST).then_inc(pad_ready, 1)
            dve.wait_ge(gate_half, 1)
            dve.tensor_scalar(gate[:, 1:2], gate[:, 1:2], 1.0 / STEPS, None, ALU.mult).then_inc(gate_ready, 1)
            with dve.Fori(0, NA - 1) as b:
                batch(b, False)
            batch(NA - 1, True)

            W = DC * TG // 2
            cur = neuron[:, 2 * W:3 * W]
            nxt = neuron[:, 3 * W:4 * W]

            def neuron_op(g, n):
                half, k = n // 13, n % 13
                y = neuron[:, half * W:(half + 1) * W]
                s = spikes[:, half * W:(half + 1) * W]
                if n == 0:
                    dve.wait_ge(y_done, g * DC + DC)
                    dve.wait_ge(spkT_mm, g * 4)
                dve.wait_ge(lif, g * LIF_OPS + n - half)
                if n == 13:
                    dve.wait_ge(spk_done, g * 2 + 1)
                if k == 0:
                    ins = dve.tensor_scalar(s, y, THRESHOLD, None, ALU.is_gt)
                elif k == 1:
                    ins = dve.scalar_tensor_tensor(nxt, y, BETA, y, ALU.mult, ALU.add)
                elif k == 2:
                    ins = dve.scalar_tensor_tensor(cur, y, THRESHOLD, nxt, ALU.is_gt, ALU.subtract)
                elif k % 3 == 0:
                    ins = dve.scalar_tensor_tensor(s, cur, -THRESHOLD, s, ALU.is_lt, ALU.add)
                elif k % 3 == 1:
                    ins = dve.scalar_tensor_tensor(nxt, cur, -BETA, y, ALU.mult, ALU.add)
                else:
                    ins = dve.scalar_tensor_tensor(cur, cur, -THRESHOLD, nxt, ALU.is_lt, ALU.subtract)
                ins.then_inc(spk_done if k == 12 else lif, 1)

            def finish(g, tiles):
                dve.wait_ge(fin_in, g * 16 + 16)
                for i in tiles:
                    dve.wait_ge(spkT_mm, g * 4 + (i + 1))
                    bank = (work[2], heads_out)[i % 2][:, 0:D // 2].bitcast(BF16)
                    dve.scalar_tensor_tensor(fin[0:LT, i, :], bank[0:LT, :], gate[0:LT, 1:2],
                                             fin[0:LT, i, :], ALU.mult, ALU.add).then_inc(fin_done, 1)

            def group_lo(g):
                for i in range(4):
                    dve.wait_ge(z_hi, g * 4 + (i + 1))
                    dve.tensor_tensor(zT[:, 1, :, i * LT:(i + 1) * LT],
                                      (work[2], heads_out)[i % 2][:, 0:TG].rearrange("p (k r) -> p k r", k=DC),
                                      zT[:, 0, :, i * LT:(i + 1) * LT].bitcast(F32),
                                      ALU.subtract).then_inc(z_lo, 1)

            def group(g, first, last):
                for j in range(FC):
                    dve.wait_ge(h_hi, g * FC + (j + 1))
                    dve.tensor_tensor(hT[:, j % 3, 1, :], h32[:, j % 2, :], hT[:, j % 3, 0, :].bitcast(F32),
                                      ALU.subtract).then_inc(h_lo, 1)
                    if first:
                        split_weights(*WITH[j])
                    elif j < 12:
                        for n in range(26 * j // 12, 26 * (j + 1) // 12):
                            neuron_op(g - 1, n)
                    elif j in (13, 14):
                        finish(g - 1, (0, 1) if j == 13 else (2, 3))
                    if not last and j == 12:
                        group_statistics(g + 1)
                    if not last and j == 13:
                        group_centre(g + 1)
                if not last:
                    group_lo(g + 1)

            group_lo(0)
            split_weights(*AT_START)
            group(0, True, False)
            with dve.Fori(1, GROUPS - 1) as g:
                group(g, False, False)
            group(GROUPS - 1, False, True)
            for n in range(26):
                neuron_op(GROUPS - 1, n)
            finish(GROUPS - 1, range(4))

        @block.gpsimd
        def _(pool):
            def all_max(b, h):
                pool.wait_ge(max_done, b * HEADS + (h + 1))
                pool.wait_ge(sub_done, (b * HEADS + max(h - 1, 0)) * 2)
                pool.tensor_tensor(tick[:, 1 + h % 2:2 + h % 2], halfneg[:, 0:1], halfneg[:, 0:1], ALU.mult)
                pool.partition_all_reduce(mxb[:, h % 2, :], mx[:, h % 2, :], P, RMAX).then_inc(maxb_done, 1)

            def denominators(b, h):
                total = dsum[:, h % 4, :]
                tile = lambda t: probs[0:ROWS[t], h % 4, t * L:(t + 1) * L]
                n = (b * HEADS + h) * (TILES - 2)
                pool.wait_ge(exp_done, b * HEADS + (h + 1))
                pool.tensor_tensor(total[0:CT, :], tile(0), tile(1), ALU.add).then_inc(dchain, 1)
                for t in range(2, TILES):
                    pool.wait_ge(dchain, n + (t - 1))
                    pool.tensor_tensor(total[0:ROWS[t], :], total[0:ROWS[t], :], tile(t),
                                       ALU.add).then_inc(dchain if t < TILES - 1 else dsum_done, 1)

            def inverse_root(ready, n, done, lo, hi):
                pool.wait_ge(ready, n)
                pool.tensor_tensor(rstd[:, lo:hi], ve[:, lo:hi], halfneg[:, lo:hi], ALU.pow).then_inc(done, 1)

            def gain_offset(b, *ts):
                for t in ts:
                    r, g = ROWS[t], 0 if t < CTX_TILES else 2
                    n = b * TILES + (t + 1)
                    pool.wait_ge(centred, n)
                    pool.tensor_tensor(xin[0:r, t, :], xin[0:r, t, :], affine[0:r, g, :], ALU.mult
                                       ).then_inc(gain_done, 1)
                    pool.wait_ge(gain_done, n)
                    pool.tensor_tensor(xin[0:r, t, :], xin[0:r, t, :], affine[0:r, g + 1, :], ALU.add
                                       ).then_inc(ln_done, 1)

            def layer_norms(b):
                inverse_root(ve_done, b * 3 + 1, rstd_done, 0, 4)
                inverse_root(ve_done, b * 3 + 2, rstd_done, 4, 8)
                gain_offset(b, 0, 1, 2, 3, 4, 5)
                inverse_root(ve_done, b * 3 + 3, rstd_done, 8, 10)
                gain_offset(b, 6, 7)

            def batch(b, last):
                all_max(b, 0)
                all_max(b, 1)
                denominators(b, 0)
                all_max(b, 2)
                all_max(b, 3)
                denominators(b, 1)
                denominators(b, 2)
                if not last:
                    layer_norms(b + 1)
                denominators(b, 3)
                all_max(b, 4)
                all_max(b, 5)
                denominators(b, 4)
                denominators(b, 5)
                all_max(b, 6)
                all_max(b, 7)
                denominators(b, 6)
                denominators(b, 7)

            pool.memset(ident[:, :], 0.0).then_inc(ident_ready, 1)
            pool.memset(ident_b[:, :], 0.0).then_inc(ident_ready, 1)
            pool.wait_ge(ident_ready, 2)
            for m in (ident, ident_b):
                pool.affine_select(out=m[:, :], in_=m[:, :], compare_op=ALU.not_equal, fill=1.0, base=0,
                                   pattern=[[-1, P]], channel_multiplier=1).then_inc(ident_ready, 1)
            pool.wait_ge(const_ready, 3)
            inverse_root(ve_done, 1, rstd_done, 0, 4)
            pool.wait_ge(affine_in, 64)
            gain_offset(0, 0, 1, 2, 3)
            inverse_root(ve_done, 2, rstd_done, 4, 8)
            gain_offset(0, 4, 5)
            inverse_root(ve_done, 3, rstd_done, 8, 10)
            gain_offset(0, 6, 7)
            with pool.Fori(0, NA - 1) as b:
                batch(b, False)
            batch(NA - 1, True)

            def squares(g, j):
                pool.wait_ge(relu_done, g * FC + (j + 1))
                pool.wait_ge(h_lo, g * FC + max(j - 1, 0))
                pool.tensor_tensor(h32[:, j % 2, :], relu[:, j % 2, :], relu[:, j % 2, :],
                                   ALU.mult).then_inc(h_done, 1)

            def group(g, last):
                for j in range(FC):
                    squares(g, j)
                    if not last and j == FC - 3:
                        inverse_root(g_ve, g + 2, g_rstd, 0, 4)

            inverse_root(g_ve, 1, g_rstd, 0, 4)
            with pool.Fori(0, GROUPS - 1) as g:
                group(g, False)
            group(GROUPS - 1, True)


_ORDER = ["x", "ctx_1024", "g_xattn", "g_ffn", "L0_xattn_Wq", "L0_xattn_Wkv", "L0_xattn_Wout", "L0_xattn_gm",
          "L0_xattn_bm", "L0_xattn_gl", "L0_xattn_bl", "L0_ffn_W_fc", "L0_ffn_W_proj"]


def kernel(**inputs):
    import numpy as np
    import concourse.bacc as bacc
    from concourse import mybir as mb
    from concourse.bass_utils import run_bass_kernel_spmd

    def laid_out(name):
        a = np.asarray(inputs[name])
        if name in ("g_xattn", "g_ffn"):
            a = np.repeat(a.reshape(1, 1), 128, axis=0)
        elif name.startswith("L0_ffn"):
            a = a.T
        return np.ascontiguousarray(a)

    nc = bacc.Bacc("TRN2", target_bir_lowering=False, num_devices=1)
    arrays, args = {}, []
    for name in _ORDER:
        a = laid_out(name)
        arrays[f"in_{name}"] = a
        args.append(nc.dram_tensor(f"in_{name}", a.shape, mb.dt.from_np(a.dtype), kind="ExternalInput").ap())
    shape = np.asarray(inputs["x"]).shape
    args.append(nc.dram_tensor("out", shape, mb.dt.float32, kind="ExternalOutput").ap())
    flamingo_block(nc, *args)
    r = run_bass_kernel_spmd(nc, [arrays], core_ids=[0])
    return r.results[0]["out"]
```

```python
from contextlib import ExitStack

import concourse.bass as bass
from concourse import mybir

F32 = mybir.dt.float32
F32R = mybir.dt.float32r
BF16 = mybir.dt.bfloat16
ALU = mybir.AluOpType
ACT = mybir.ActivationFunctionType
AX = mybir.AxisListType
RMAX = bass.bass_isa.ReduceOp.max

P = 128
EPS = 1e-5
LOWEST = -3.0e38
BETA = 0.9
THRESHOLD = 1.0
STEPS = 5


def flamingo_block(nc, x, ctx_in, g_xattn, g_ffn, Wq, Wkv, Wout, gm, bm, gl, bl, WfcT, WprojT, out):
    B, L, D = x.shape
    T = ctx_in.shape[1]
    F = WfcT.shape[1]
    DH = 64
    HEADS = D // DH
    DC = D // P
    LT = L // 2
    CTX_TILES = 6
    CT = T // CTX_TILES
    TILES = CTX_TILES + 2
    KEYS = T + L
    HALF = (KEYS // 2 + 1) // 2 * 2
    PAIRS = HEADS // 2
    QSCALE = float(DH) ** 0.5
    ROWS = [CT] * CTX_TILES + [LT] * 2
    AT = [t * CT for t in range(CTX_TILES)] + [T, T + LT]
    BANKS = TILES // 2
    PASSES = ((0, 0), (0, 1), (1, 0))
    TG = 512
    GROUPS = -(-B * L // TG)
    LAST_TG = B * L - (GROUPS - 1) * TG
    FC = F // P
    assert CT * CTX_TILES == T and CT <= P and HALF <= 512 and D == 512
    assert 0 < LAST_TG <= TG // 2 and DC == 4 and LAST_TG % P == 0

    x_flat = x.rearrange("b l d -> (b l) d")
    out_flat = out.rearrange("b l d -> (b l) d")
    x1_dram = nc.dram_tensor("x1_scratch", (B * L, D), F32, kind="Internal").ap()

    keep = ExitStack()
    with keep:
        def sb(stack, name, shape, dt=F32):
            return stack.enter_context(nc.sbuf_tensor(name, shape, dt))

        def sem(name):
            return keep.enter_context(nc.semaphore(name))

        ident = sb(keep, "ident", [P, P])
        ident_b = sb(keep, "ident_b", [P, P], BF16)
        ones = sb(keep, "ones", [P, DH])
        gate_in = sb(keep, "gate_in", [P, 2])
        gate = sb(keep, "gate", [P, 2])
        halfneg = sb(keep, "halfneg", [P, TILES])
        bn = sb(keep, "bn", [P, TILES, 6])
        mv = sb(keep, "mv", [P, TILES, 2])
        ve = sb(keep, "ve", [P, TILES])
        rstd = sb(keep, "rstd", [P, TILES])
        tick = sb(keep, "tick", [P, 3])

        score = keep.enter_context(nc.psum_tensor("score", [P, BANKS, 512], F32))
        work = [keep.enter_context(nc.psum_tensor(f"work{i}", [P, 512], F32)) for i in range(3)]
        heads_out = keep.enter_context(nc.psum_tensor("heads_out", [P, 512], F32))

        a = ExitStack()
        affine = sb(a, "affine", [P, 4, D])
        xin = sb(a, "xin", [P, TILES, D])
        wq = sb(a, "wq", [P, 2, DC, D], F32R)
        wk = sb(a, "wk", [P, 2, DC, D], F32R)
        wv = sb(a, "wv", [P, 2, DC, D], F32R)
        xT = sb(a, "xT", [P, 2, DC, KEYS], F32R)
        kst = sb(a, "kst", [P, 2, 2, KEYS], F32R)
        qst = sb(a, "qst", [P, 2, 2, 2, L], F32R)
        vals = sb(a, "vals", [P, TILES, D])
        probs = sb(a, "probs", [P, 4, TILES * L])
        mx = sb(a, "mx", [P, 2, L])
        mxb = sb(a, "mxb", [P, 2, L])
        dsum = sb(a, "dsum", [P, 4, L])
        on32 = sb(a, "on32", [P, L])
        oT = sb(a, "oT", [P, 2, PAIRS, L], F32R)
        wo = sb(a, "wo", [P, 2, DC, D], F32R)
        xres = sb(a, "xres", [P, 2, D])
        a.close()

        bb = ExitStack()
        zt = sb(bb, "zt", [P, 4, D])
        zT = sb(bb, "zT", [P, 2, DC, TG], F32R)
        wf = sb(bb, "wf", [P, 2, FC, DC * P], F32R)
        neuron = sb(bb, "neuron", [P, 2 * DC * TG])
        wp = sb(bb, "wp", [P, 2, FC, D], F32R)
        relu = sb(bb, "relu", [P, 2, TG])
        h32 = sb(bb, "h32", [P, 2, TG])
        fin = sb(bb, "fin", [P, 4, D])
        hT = sb(bb, "hT", [P, 3, 2, TG], F32R)
        spikes = sb(bb, "spikes", [P, DC * TG], BF16)
        bb.close()

        EARLY = 8
        SLOTS = 8
        PIECES = [("up", j) for j in range(EARLY)]
        for j in range(FC):
            PIECES.append(("down", j))
            if j + EARLY < FC:
                PIECES.append(("up", j + EARLY))

        WITH = [range(EARLY + 2 * j, min(EARLY + 2 * j + 2, len(PIECES))) for j in range(FC)]
        assert sum(map(len, WITH)) + EARLY == len(PIECES)

        def stage(n):
            return neuron[:, n % SLOTS * 512:(n % SLOTS + 1) * 512]

        def piece(n, part):
            kind, j = PIECES[n]
            return (wf if kind == "up" else wp)[:, part, j, :]

        def tiles_of(last):
            return (LAST_TG if last else TG) // P

        def fin_of(last):
            return zt[:, 4 - LAST_TG // P:, :] if last else fin[:, :, :]

        def group_rows(d, g, last):
            if last:
                return d[(GROUPS - 1) * TG:, :].rearrange("(i r) d -> r i d", r=P)
            return d[0:(GROUPS - 1) * TG, :].rearrange("(g i r) d -> g r i d", g=GROUPS - 1, r=P)[g]

        def z_bank(g, i):
            return tile_bank(i) if isinstance(g, int) and g == 0 else (work[2], heads_out)[i % 2]

        def kq_bank(c, u):
            return work[((25, 0, 11, 14)[c] + u) % 3]

        def tile_bank(t):
            return work[(t + 2) % 3]

        def out_bank(i):
            return work[(28 + i) % 3]

        def up_bank(g, j):
            return score[:, DC - 1, :] if isinstance(g, int) and (g, j) == (0, 1) else work[j % 2]

        def spikes_of(last, half):
            if last:
                return relu[:, half, TG - LAST_TG:].bitcast(BF16)
            return spikes[:, half * (DC * TG // 2):(half + 1) * (DC * TG // 2)]

        ident_ready = sem("ident_ready")
        const_ready = sem("const_ready")
        small_in = sem("small_in")
        affine_in = [sem(f"affine_in{i}") for i in range(2)]
        gate_ready = sem("gate_ready")
        gate_half = sem("gate_half")
        w_in = [sem(f"w_in{i}") for i in range(4)]
        w_hi = sem("w_hi")
        w_lo = [sem(f"w_lo{i}") for i in range(4)]
        pad_ready = sem("pad_ready")
        x_in = [sem(f"x_in{i}") for i in range(TILES)]
        bn_done = sem("bn_done")
        mv_done = sem("mv_done")
        ve_done = sem("ve_done")
        rstd_done = sem("rstd_done")
        gain_done = sem("gain_done")
        scaled = sem("scaled")
        ln_done = sem("ln_done")
        ln_first = sem("ln_first")
        tr_done = sem("tr_done")
        xhi_done = sem("xhi_done")
        xlo_done = sem("xlo_done")
        kq_mm = sem("kq_mm")
        kq_hi = sem("kq_hi")
        q_both = sem("q_both")
        kq_done = sem("kq_done")
        v_mm = sem("v_mm")
        v_done = sem("v_done")
        s_mm = sem("s_mm")
        s_copied = sem("s_copied")
        max_done = sem("max_done")
        maxb_done = sem("maxb_done")
        sub_done = sem("sub_done")
        sub_latents = sem("sub_latents")
        exp_done = sem("exp_done")
        dchain = sem("dchain")
        dsum_done = sem("dsum_done")
        dve_dchain = sem("dve_dchain")
        dve_dsum_done = sem("dve_dsum_done")
        pv_done = sem("pv_done")
        rden_done = sem("rden_done")
        on_done = sem("on_done")
        ohi_done = sem("ohi_done")
        o_done = sem("o_done")
        wo_mm = sem("wo_mm")
        x1_done = sem("x1_done")
        res_in = [sem(f"res_in{i}") for i in range(2)]
        x1_out = [sem(f"x1_out{i}") for i in range(2)]
        fw_in = [sem(f"fw_in{i}") for i in range(SLOTS)]
        fw_hi = sem("fw_hi")
        fw_lo = sem("fw_lo")
        zt_in = sem("zt_in")
        fin_in = sem("fin_in")
        last_fin_in = sem("last_fin_in")
        g_bn = sem("g_bn")
        g_mv = sem("g_mv")
        g_ve = sem("g_ve")
        g_rstd = sem("g_rstd")
        z_done = sem("z_done")
        zt_mm = sem("zt_mm")
        z_hi = sem("z_hi")
        z_lo = sem("z_lo")
        up_mm = sem("up_mm")
        relu_done = sem("relu_done")
        h_done = sem("h_done")
        h_hi = sem("h_hi")
        h_lo = sem("h_lo")
        down_mm = sem("down_mm")
        y_mm = sem("y_mm")
        y_done = sem("y_done")
        lif = sem("lif")
        spk_done = sem("spk_done")
        spkT_mm = sem("spkT_mm")
        fin_scaled = sem("fin_scaled")
        fin_done = sem("fin_done")
        last_fin_done = sem("last_fin_done")
        fin_out = sem("fin_out")

        block = keep.enter_context(nc.Block())

        def tile_src(b, t):
            if t < CTX_TILES:
                return ctx_in[b, AT[t]:AT[t] + CT, :]
            return x[b, (t - CTX_TILES) * LT:(t - CTX_TILES + 1) * LT, :]

        NA = B
        staged = [vals[:, (i % 2) * DC:(i % 2 + 1) * DC, :] for i in range(4)]
        LIF_OPS = 24

        @block.sync
        def _(sp):
            def load_tile(b, t):
                sp.dma_start(xin[0:ROWS[t], t, :], tile_src(b, t)).then_inc(x_in[t], 16)

            def load_residual(b, i):
                sp.dma_start(xres[0:LT, i, :], x[b, i * LT:(i + 1) * LT, :]).then_inc(res_in[i], 16)

            def refill(b):
                for t in range(TILES):
                    sp.wait_ge(tr_done, b * TILES + (t + 1))
                    load_tile(b + 1, t)

            def residual(b, last):
                for i in range(2):
                    sp.wait_ge(x1_done, b * 2 + (i + 1))
                    rows = x1_dram.rearrange("(b i r) d -> b i r d", b=B, i=2)[b, i]
                    sp.dma_start(rows, xres[0:LT, i, :]).then_inc(x1_out[i], 16)
                    sp.wait_ge(x1_out[i], b * 16 + 16)
                    if not last:
                        load_residual(b + 1, i)

            def load_weight(i, w, at):
                sp.dma_start(at, w.rearrange("(k p) n -> p k n", p=P)).then_inc(w_in[i], 16)

            def load_affine(i, *vectors):
                for j, v in enumerate(vectors):
                    sp.dma_start(affine[:, 2 * i + j, :], v.partition_broadcast(P)).then_inc(affine_in[i], 16)

            for t in range(4):
                load_tile(0, t)
            load_affine(0, gm, bm)
            for t in range(4, TILES):
                load_tile(0, t)
            load_weight(0, Wkv[:, 0:D], staged[0])
            load_affine(1, gl, bl)
            load_weight(1, Wq, staged[1])
            sp.wait_ge(w_lo[0], 1)
            load_weight(2, Wkv[:, D:2 * D], staged[2])
            sp.wait_ge(w_lo[1], 1)
            load_weight(3, Wout, staged[3])
            sp.dma_start(gate_in[:, 0:1], g_xattn).then_inc(small_in, 16)
            sp.dma_start(gate_in[:, 1:2], g_ffn).then_inc(small_in, 16)
            for i in range(2):
                load_residual(0, i)
            refill(0)
            with sp.Fori(1, NA - 1) as b:
                refill(b)
                residual(b - 1, False)
            residual(NA - 2, False)

            def load_z(g, last):
                sp.dma_start(zt[:, 0:tiles_of(last), :], group_rows(x1_dram, g, last)).then_inc(zt_in, 16)

            def load_fin(g, last):
                sp.dma_start(fin_of(last), group_rows(x1_dram, g, last)).then_inc(last_fin_in if last else fin_in, 16)

            def store_fin(g, last):
                for i in range(tiles_of(last)):
                    if last:
                        sp.wait_ge(last_fin_done, i + 1)
                    else:
                        sp.wait_ge(fin_done, g * 4 + (i + 1))
                    rows = out_flat.rearrange("(t r) d -> t r d", r=P)[g * 4 + i]
                    sp.dma_start(rows, fin_of(last)[:, i, :]).then_inc(fin_out, 16)

            def group(g, next_last):
                sp.wait_ge(zt_mm, g * 4 + 4)
                load_z(g + 1, next_last)
                store_fin(g - 1, False)
                sp.wait_ge(fin_out, g * 64)
                load_fin(g, False)

            def load_piece(n):
                kind, j = PIECES[n]
                if n >= SLOTS:
                    sp.wait_ge(fw_lo, n - SLOTS + 1)
                if kind == "up":
                    sp.dma_start(stage(n).rearrange("p (k f) -> p k f", k=DC),
                                 WfcT.rearrange("(k p) (j f) -> j p k f", p=P, f=P)[j]).then_inc(fw_in[n % SLOTS], 16)
                else:
                    sp.dma_start(stage(n), WprojT[j * P:(j + 1) * P, :]).then_inc(fw_in[n % SLOTS], 16)

            sp.wait_ge(tr_done, NA * TILES)
            load_z(0, False)
            sp.wait_ge(kq_mm, NA * 12)
            sp.wait_ge(v_mm, NA * TILES)
            for n in range(SLOTS - 1):
                load_piece(n)
            sp.wait_ge(s_mm, NA * HEADS * BANKS)
            load_piece(SLOTS - 1)
            for n in range(SLOTS, SLOTS + EARLY):
                load_piece(n)
            residual(NA - 1, True)
            load_fin(0, False)
            for n in range(SLOTS + EARLY, len(PIECES)):
                load_piece(n)
            sp.wait_ge(zt_mm, 4)
            load_z(1, False)
            with sp.Fori(1, GROUPS - 2) as g:
                group(g, False)
            group(GROUPS - 2, True)
            load_fin(GROUPS - 1, True)
            store_fin(GROUPS - 2, False)
            store_fin(GROUPS - 1, True)
            sp.wait_ge(fin_out, (GROUPS - 1) * 64 + LAST_TG // P * 16)

        @block.tensor
        def _(pe):
            def product(bank, lhs, rhs, chunks, passes=PASSES):
                n = 0
                for i, j in passes:
                    for k in range(chunks):
                        mm = pe.matmul(bank, lhs(i, k), rhs(j, k), start=(n == 0),
                                       stop=(n == len(passes) * chunks - 1))
                        n += 1
                return mm

            def transposes(b, t, first):
                if t < 3:
                    if not first:
                        pe.wait_ge(kq_done, b * 12 - 2 + t)
                else:
                    pe.wait_ge(xlo_done, b * TILES + (t - 2))
                if first and t >= 4:
                    pe.wait_ge(ln_first, t - 3)
                elif first:
                    pe.wait_ge(ln_done, t + 1)
                else:
                    pe.wait_ge(ln_done, b * TILES + (t - 3))
                bank = tile_bank(t)
                for k in range(DC):
                    mm = pe.transpose(bank[:, k * P:k * P + ROWS[t]], xin[0:ROWS[t], t, k * P:(k + 1) * P],
                                      ident[0:ROWS[t], 0:ROWS[t]])
                mm.then_inc(tr_done, 1)

            def keys_queries(b, c, us=range(3)):
                cols = slice(c * P, (c + 1) * P)
                for u in us:
                    if c == 0:
                        pe.wait_ge(xlo_done, b * TILES + (6 if u == 0 else 8))
                    elif c == 1:
                        pe.wait_ge(kq_done, b * 12 + 3)
                        if u > 0:
                            pe.wait_ge(x1_done, b * 2)
                    elif c == 2:
                        pe.wait_ge(v_done, b * TILES + (6 + u))
                    else:
                        pe.wait_ge(kq_done, b * 12 + (7 + u))
                    bank = kq_bank(c, u)
                    if u < 2:
                        lo, hi = (0, HALF) if u == 0 else (HALF, KEYS)
                        mm = product(bank[:, 0:hi - lo], lambda i, k: wk[:, i, k, cols],
                                     lambda i, k: xT[:, i, k, lo:hi], DC)
                    else:
                        mm = product(bank[:, 0:L], lambda i, k: wq[:, i, k, cols],
                                     lambda i, k: xT[:, i, k, T:KEYS], DC)
                    mm.then_inc(kq_mm, 1)

            def values(b, t):
                if t == 0:
                    pe.wait_ge(w_lo[2], 1)
                if t < 3:
                    pe.wait_ge(kq_done, b * 12 + (4 + t))
                else:
                    pe.wait_ge(v_done, b * TILES + (t - 2))
                product(work[t % 3][0:ROWS[t], :], lambda i, k: xT[:, i, k, AT[t]:AT[t] + ROWS[t]],
                        lambda i, k: wv[:, i, k, :], DC).then_inc(v_mm, 1)

            def scores(b, h):
                s, e = h // 2 % 2, h % 2
                pe.wait_ge(q_both, b * 8 + (2 * (h // 2) + 2))
                for t in range(TILES):
                    if t % 2 == 0:
                        pe.wait_ge(s_copied, (b * HEADS + h) * BANKS - (BANKS - 1 - t // 2 if h else 0))
                    for j in range(2):
                        mm = pe.matmul(score[0:ROWS[t], t // 2, t % 2 * L:(t % 2 + 1) * L],
                                       kst[:, s, e, AT[t]:AT[t] + ROWS[t]], qst[:, s, j, e, :],
                                       start=(j == 0), stop=(j == 1))
                    if t % 2:
                        mm.then_inc(s_mm, 1)

            def attend(b, p, between=None):
                pe.wait_ge(v_done, b * TILES + TILES)
                pe.wait_ge(o_done, b * PAIRS + p)
                pe.wait_ge(exp_done, b * HEADS + (2 * p + 2))
                for t in range(TILES):
                    for e in range(2):
                        h = 2 * p + e
                        pe.matmul(heads_out[e * DH:(e + 1) * DH, 0:L], vals[0:ROWS[t], t, h * DH:(h + 1) * DH],
                                  probs[0:ROWS[t], h % 4, t * L:(t + 1) * L],
                                  start=(t == 0), stop=(t == TILES - 1))
                if between:
                    between()
                pe.wait_ge(dsum_done, b * (HEADS - 2) + (2, 4, 5, 6)[p])
                if p >= 2:
                    pe.wait_ge(dve_dsum_done, b * 2 + (p - 1))
                for e in range(2):
                    mm = pe.matmul(heads_out[e * DH:(e + 1) * DH, L:2 * L], ones[0:CT, :],
                                   dsum[0:CT, (2 * p + e) % 4, :], start=True, stop=True)
                mm.then_inc(pv_done, 1)

            def out_projection(b, pairs, last):
                if pairs[0] == 0:
                    pe.wait_ge(w_lo[3], 1)
                pe.wait_ge(o_done, b * PAIRS + pairs[-1] + 1)
                for i in range(2):
                    if pairs[0] == 0:
                        if last:
                            pe.wait_ge(z_lo, 4)
                        else:
                            pe.wait_ge(kq_done, b * 12 + (13 + i))
                    for p in pairs:
                        for n, (m, k) in enumerate(PASSES):
                            mm = pe.matmul(out_bank(i)[0:LT, :], oT[:, m, p, i * LT:(i + 1) * LT],
                                           wo[:, k, p, :], start=(p == 0 and n == 0),
                                           stop=(p == PAIRS - 1 and n == 2))
                    if pairs[-1] == PAIRS - 1:
                        mm.then_inc(wo_mm, 1)

            def group_transpose(g, i):
                pe.wait_ge(z_done, g * 4 + (i + 1))
                bank = z_bank(g, i)
                for k in range(DC):
                    mm = pe.transpose(bank[:, k * P:(k + 1) * P], zt[:, i, k * P:(k + 1) * P], ident[:, :])
                mm.then_inc(zt_mm, 1)

            def up(g, j, last):
                n = LAST_TG if last else TG
                if j < 2:
                    pe.wait_ge(relu_done, g * FC)
                else:
                    pe.wait_ge(relu_done, g * FC + (j - 1))
                pe.wait_ge(fw_lo, PIECES.index(("up", j)) + 1)
                product(up_bank(g, j)[:, 0:n], lambda i, k: wf[:, i, j, k * P:(k + 1) * P],
                        lambda i, k: zT[:, i, k, 0:n], DC).then_inc(up_mm, 1)

            def batch(b, last):
                def ahead(*ts):
                    for t in ts:
                        if not last:
                            transposes(b + 1, t, False)
                        elif t < 4:
                            if t < 3:
                                pe.wait_ge(kq_done, NA * 12 - 2 + t)
                            else:
                                pe.wait_ge(z_lo, t - 2)
                            group_transpose(0, t)

                keys_queries(b, 1, (1, 2))
                values(b, 0)
                values(b, 1)
                scores(b, 2)
                values(b, 2)
                scores(b, 3)
                for t in range(3, TILES):
                    values(b, t)
                keys_queries(b, 2)
                attend(b, 0)
                scores(b, 4)
                scores(b, 5)
                keys_queries(b, 3)
                ahead(0)
                attend(b, 1)
                ahead(1, 2)
                scores(b, 6)
                ahead(3)
                scores(b, 7)
                ahead(4, 5)
                if not last:
                    attend(b, 2, lambda: (ahead(6, 7), keys_queries(b + 1, 0, (0,))))
                    keys_queries(b + 1, 0, (1, 2))
                    out_projection(b, range(PAIRS - 1), last)
                    scores(b + 1, 0)
                    attend(b, 3)
                    keys_queries(b + 1, 1, (0,))
                    out_projection(b, range(PAIRS - 1, PAIRS), last)
                    scores(b + 1, 1)
                else:
                    pe.wait_ge(z_lo, 4)
                    up(0, 0, False)
                    attend(b, 2)
                    out_projection(b, range(PAIRS - 2), last)
                    out_projection(b, range(PAIRS - 2, PAIRS - 1), last)
                    attend(b, 3)
                    pe.wait_ge(s_copied, NA * HEADS * BANKS)
                    up(0, 1, False)
                    out_projection(b, range(PAIRS - 1, PAIRS), last)

            pe.wait_ge(ident_ready, 4)
            pe.wait_ge(const_ready, 1)
            for t in range(TILES):
                transposes(0, t, True)
            pe.wait_ge(w_lo[0], 1)
            keys_queries(0, 0, (0, 1))
            pe.wait_ge(w_lo[1], 1)
            keys_queries(0, 0, (2,))
            scores(0, 0)
            scores(0, 1)
            keys_queries(0, 1, (0,))
            with pe.Fori(0, NA - 1) as b:
                batch(b, False)
            batch(NA - 1, True)

            def group_transposes(g, last, first):
                for i in range(tiles_of(last)):
                    if i >= 2:
                        pe.wait_ge(z_lo, g * 4 + (i - 1))
                    elif not first:
                        pe.wait_ge(fin_done, g * 4 - 4)
                    group_transpose(g, i)

            def down(g, j, last):
                n_tok = LAST_TG if last else TG
                pe.wait_ge(h_lo, g * FC + (j + 1))
                if j == 0:
                    pe.wait_ge(y_done, g * DC)
                pe.wait_ge(fw_lo, PIECES.index(("down", j)) + 1)
                for d in range(DC):
                    for n, (w, a_) in enumerate(PASSES):
                        mm = pe.matmul(score[:, d, 0:n_tok], wp[:, w, j, d * P:(d + 1) * P],
                                       hT[:, j % 3, a_, 0:n_tok],
                                       start=(j == 0 and n == 0), stop=(j == FC - 1 and n == 2))
                    if j == FC - 1:
                        mm.then_inc(y_mm, 1)
                    elif d == DC - 1:
                        mm.then_inc(down_mm, 1)

            def spikes_back(g, tiles, last, read=None):
                n_tok = LAST_TG if last else TG
                pe.wait_ge(spk_done, g * 2 + 2)
                for i in tiles:
                    if read:
                        read(i)
                    bank = (work[2], heads_out)[i % 2][:, 0:D // 2].bitcast(BF16)
                    for k in range(DC):
                        mm = pe.transpose(bank[:, k * P:(k + 1) * P],
                                          spikes_of(last, k // 2)[:, k % 2 * n_tok + i * P:k % 2 * n_tok + (i + 1) * P],
                                          ident_b[:, :])
                    mm.then_inc(spkT_mm, 1)

            def group(g, first, next_last):
                pe.wait_ge(z_lo, g * 4 + 4)
                for j in range(FC):
                    if first and j == 2:
                        pe.wait_ge(relu_done, 2)
                    if first and j == 3:
                        pe.wait_ge(x1_done, NA * 2 - 1)
                    if not first or j > 1:
                        up(g, j, False)
                    if j >= 2:
                        down(g, j - 2, False)
                    if not first and j in (13, 14):
                        if j == 13:
                            spikes_back(g - 1, (0, 1), False)
                        else:
                            spikes_back(g - 1, (2, 3), False, lambda i: pe.wait_ge(fin_done, g * 4 + (i - 5)))
                if first:
                    pe.wait_ge(x1_done, NA * 2)
                group_transposes(g + 1, next_last, first)
                down(g, FC - 2, False)
                down(g, FC - 1, False)

            def last_group(g):
                pe.wait_ge(z_lo, g * 4 + LAST_TG // P)
                for j in range(FC):
                    up(g, j, True)
                    if j >= 2:
                        down(g, j - 2, True)
                down(g, FC - 2, True)
                down(g, FC - 1, True)
                spikes_back(g - 1, (0, 1), False)
                spikes_back(g - 1, (2, 3), False, lambda i: pe.wait_ge(fin_scaled, i - 1))
                spikes_back(g, range(LAST_TG // P), True, lambda i: pe.wait_ge(fin_scaled, i + 3))

            group(0, True, False)
            with pe.Fori(1, GROUPS - 2) as g:
                group(g, False, False)
            group(GROUPS - 2, False, True)
            last_group(GROUPS - 1)

        @block.scalar
        def _(act):
            def copy_scores(b, h, first=False):
                if h >= 2:
                    act.wait_ge(pv_done, b * PAIRS + h // 2 - 1)
                elif not first:
                    act.wait_ge(pv_done, b * PAIRS - 1)
                for k in range(BANKS):
                    act.wait_ge(s_mm, (b * HEADS + h) * BANKS + (k + 1))
                    r = ROWS[2 * k]
                    act.activation(probs[0:r, h % 4, 2 * k * L:(2 * k + 2) * L], score[0:r, k, 0:2 * L],
                                   ACT.Copy).then_inc(s_copied, 1)

            def exponentials(b, h):
                act.wait_ge(sub_done, b * HEADS + (h + 1))
                act.activation(probs[0:CT, h % 4, 0:CTX_TILES * L], probs[0:CT, h % 4, 0:CTX_TILES * L], ACT.Exp)
                act.wait_ge(sub_latents, b * HEADS + (h + 1))
                act.activation(probs[0:LT, h % 4, CTX_TILES * L:], probs[0:LT, h % 4, CTX_TILES * L:],
                               ACT.Exp).then_inc(exp_done, 1)

            def kq_hi_parts(b, c, *us):
                s = c % 2
                if c == 1:
                    act.wait_ge(s_mm, b * HEADS * BANKS)
                elif c >= 2:
                    act.wait_ge(s_mm, b * HEADS * BANKS + (2 * c - 2) * BANKS)
                for u in us:
                    act.wait_ge(kq_mm, b * 12 + (3 * c + u + 1))
                    bank = kq_bank(c, u)
                    for e in range(2):
                        rows = slice(e * DH, (e + 1) * DH)
                        if u < 2:
                            lo, hi = (0, HALF) if u == 0 else (HALF, KEYS)
                            act.activation(kst[rows, s, e, lo:hi], bank[rows, 0:hi - lo],
                                           ACT.Copy).then_inc(kq_hi, 1)
                        else:
                            act.activation(qst[0:DH, s, 0, e, :], bank[rows, 0:L], ACT.Copy, scale=QSCALE)
                            act.activation(qst[DH:P, s, 0, e, :], bank[rows, 0:L], ACT.Copy,
                                           scale=QSCALE).then_inc(kq_hi, 1)

            def q_lo_copies(b, c):
                s = c % 2
                act.wait_ge(kq_done, b * 12 + (3 * c + 3))
                for e in range(2):
                    rows = slice(e * DH, (e + 1) * DH)
                    other = slice((1 - e) * DH, (2 - e) * DH)
                    act.activation(qst[other, s, 1, e, :], qst[rows, s, 1, e, :].bitcast(F32),
                                   ACT.Copy).then_inc(q_both, 1)

            def scale_tiles(b, *ts):
                act.wait_ge(rstd_done, b * 2 + (ts[0] // 4 + 1))
                for t in ts:
                    act.wait_ge(gain_done, b * TILES + (t + 1))
                    r = ROWS[t]
                    act.activation(xin[0:r, t, :], xin[0:r, t, :], ACT.Copy,
                                   scale=rstd[0:r, t:t + 1]).then_inc(scaled, 1)

            def copy_values(b, *ts):
                act.wait_ge(pv_done, b * PAIRS)
                for t in ts:
                    if t % DC == 0:
                        act.wait_ge(w_lo[2 + t // DC], 1)
                    act.wait_ge(v_mm, b * TILES + (t + 1))
                    act.activation(vals[0:ROWS[t], t, :], work[t % 3][0:ROWS[t], :], ACT.Copy).then_inc(v_done, 1)

            def hi_tile(b, t):
                if t == 0:
                    act.wait_ge(kq_mm, b * 12)
                act.wait_ge(tr_done, b * TILES + (t + 1))
                act.activation(xT[:, 0, :, AT[t]:AT[t] + ROWS[t]],
                               tile_bank(t)[:, :].rearrange("p (k r) -> p k r", k=DC)[:, :, 0:ROWS[t]],
                               ACT.Copy).then_inc(xhi_done, 1)

            def group_hi(g, *tiles):
                for i in tiles:
                    act.wait_ge(zt_mm, g * 4 + (i + 1))
                    act.activation(zT[:, 0, :, i * P:(i + 1) * P],
                                   z_bank(g, i)[:, :].rearrange("p (k r) -> p k r", k=DC),
                                   ACT.Copy).then_inc(z_hi, 1)

            def split_weights(*pieces):
                for n in pieces:
                    act.wait_ge(fw_in[n % SLOTS], 16 * (n // SLOTS + 1))
                    act.activation(piece(n, 0), stage(n), ACT.Copy).then_inc(fw_hi, 1)

            def batch(b, last):
                def ahead(*ts):
                    for t in ts:
                        if not last:
                            hi_tile(b + 1, t)
                        elif t < 4:
                            group_hi(0, t)

                kq_hi_parts(b, 1, 1)
                exponentials(b, 0)
                kq_hi_parts(b, 1, 2)
                q_lo_copies(b, 1)
                copy_values(b, 0, 1)
                copy_scores(b, 2)
                exponentials(b, 1)
                copy_values(b, 2)
                copy_scores(b, 3)
                copy_values(b, 3, 4)
                if not last:
                    scale_tiles(b + 1, 0, 1)
                copy_values(b, 5)
                exponentials(b, 2)
                copy_values(b, 6)
                exponentials(b, 3)
                copy_values(b, 7)
                if not last:
                    scale_tiles(b + 1, 2, 3)
                kq_hi_parts(b, 2, 0, 1, 2)
                q_lo_copies(b, 2)
                if not last:
                    scale_tiles(b + 1, 4, 5)
                copy_scores(b, 4)
                copy_scores(b, 5)
                if not last:
                    scale_tiles(b + 1, 6, 7)
                kq_hi_parts(b, 3, 0, 1, 2)
                exponentials(b, 4)
                q_lo_copies(b, 3)
                ahead(0, 1, 2)
                if last:
                    split_weights(0)
                copy_scores(b, 6)
                if last:
                    ahead(3)
                    exponentials(b, 5)
                else:
                    exponentials(b, 5)
                    ahead(3)
                copy_scores(b, 7)
                ahead(4, 5, 6, 7)
                if not last:
                    kq_hi_parts(b + 1, 0, 0, 1, 2)
                    q_lo_copies(b + 1, 0)
                    exponentials(b, 6)
                    exponentials(b, 7)
                    copy_scores(b + 1, 0)
                    kq_hi_parts(b + 1, 1, 0)
                    copy_scores(b + 1, 1)
                else:
                    split_weights(1)
                    exponentials(b, 6)
                    exponentials(b, 7)
                    split_weights(*range(2, EARLY))

            def split_hi(i, w):
                act.wait_ge(w_in[i], 16)
                act.activation(w[:, 0], staged[i], ACT.Copy).then_inc(w_hi, 1)

            scale_tiles(0, 0, 1, 2, 3)
            split_hi(0, wk)
            hi_tile(0, 0)
            scale_tiles(0, 4, 5)
            hi_tile(0, 1)
            scale_tiles(0, 6, 7)
            hi_tile(0, 2)
            hi_tile(0, 3)
            for t in range(4, TILES):
                hi_tile(0, t)
            split_hi(1, wq)
            kq_hi_parts(0, 0, 0, 1, 2)
            q_lo_copies(0, 0)
            split_hi(2, wv)
            act.wait_ge(pad_ready, 2)
            copy_scores(0, 0, True)
            split_hi(3, wo)
            act.wait_ge(small_in, 32)
            act.activation(gate[:, :], gate_in[:, :], ACT.Tanh).then_inc(gate_half, 1)
            kq_hi_parts(0, 1, 0)
            copy_scores(0, 1, True)
            with act.Fori(0, NA - 1) as b:
                batch(b, False)
            batch(NA - 1, True)

            def group(g, first, last, next_last):
                n_tok = LAST_TG if last else TG
                for j in range(FC):
                    if not first or j > 1:
                        now = (j,)
                    else:
                        now = (0, 1) if j == 0 else ()
                    for i in now:
                        act.wait_ge(up_mm, g * FC + (i + 1))
                        if i < 2:
                            act.wait_ge(h_done, g * FC)
                        else:
                            act.wait_ge(h_done, g * FC + (i - 1))
                        act.activation(relu[:, i % 2, 0:n_tok], up_bank(g, i)[:, 0:n_tok],
                                       ACT.Relu).then_inc(relu_done, 1)
                    act.wait_ge(h_done, g * FC + (j + 1))
                    if first and j == 0:
                        act.wait_ge(wo_mm, NA * 2)
                    if j < 3:
                        act.wait_ge(y_mm, g * DC)
                    else:
                        act.wait_ge(down_mm, g * (FC - 1) + (j - 2))
                    act.activation(hT[:, j % 3, 0, 0:n_tok], h32[:, j % 2, 0:n_tok], ACT.Copy).then_inc(h_hi, 1)
                    if first:
                        split_weights(*WITH[j])
                if not last:
                    group_hi(g + 1, *range(tiles_of(next_last)))
                act.wait_ge(spk_done, g * 2)
                act.wait_ge(fw_lo, len(PIECES))
                for d in range(DC):
                    act.wait_ge(y_mm, g * DC + (d + 1))
                    act.activation(neuron[:, d * n_tok:(d + 1) * n_tok], score[:, d, 0:n_tok],
                                   ACT.Copy).then_inc(y_done, 1)

            act.wait_ge(pv_done, NA * PAIRS)
            group(0, True, False, False)
            with act.Fori(1, GROUPS - 2) as g:
                group(g, False, False, False)
            group(GROUPS - 2, False, False, True)
            group(GROUPS - 1, False, True, False)
            act.wait_ge(gate_ready, 1)
            for i in range(4):
                act.wait_ge(spkT_mm, (GROUPS - 2) * 4 + (i + 1))
                if i >= 2:
                    act.wait_ge(fin_done, (GROUPS - 2) * 4 + (i - 1))
                act.activation(zt[:, i % 2, :], (work[2], heads_out)[i % 2][:, 0:D // 2].bitcast(BF16), ACT.Copy,
                               scale=gate[:, 1:2]).then_inc(fin_scaled, 1)

        @block.vector
        def _(dve):
            def scale_max(b, h):
                dve.wait_ge(s_copied, (b * HEADS + h + 1) * BANKS)
                dve.wait_ge(maxb_done, b * HEADS + max(h - 1, 0))
                dve.tensor_reduce(mx[0:CT, h % 2, :],
                                  probs[0:CT, h % 4, :].rearrange("p (t l) -> p l t", t=TILES),
                                  AX.X, ALU.max).then_inc(max_done, 1)

            def subtract(b, h):
                dve.wait_ge(maxb_done, b * HEADS + (h + 1))
                v = probs[0:CT, h % 4, 0:CTX_TILES * L].rearrange("p (t l) -> p t l", t=CTX_TILES)
                dve.tensor_tensor(v, v, mxb[0:CT, h % 2:h % 2 + 1, :].to_broadcast([CT, CTX_TILES, L]),
                                  ALU.subtract).then_inc(sub_done, 1)

            def kq_lo_parts(b, c, us=range(3)):
                s = c % 2
                for u in us:
                    bank = kq_bank(c, u)
                    for e in range(2):
                        rows = slice(e * DH, (e + 1) * DH)
                        other = slice((1 - e) * DH, (2 - e) * DH)
                        dve.wait_ge(kq_hi, (b * 12 + (3 * c + u)) * 2 + (e + 1))
                        if u < 2:
                            lo, hi = (0, HALF) if u == 0 else (HALF, KEYS)
                            ins = dve.tensor_tensor(kst[other, s, e, lo:hi], bank[rows, 0:hi - lo],
                                                    kst[rows, s, e, lo:hi].bitcast(F32), ALU.subtract)
                        else:
                            ins = dve.scalar_tensor_tensor(qst[rows, s, 1, e, :], bank[rows, 0:L], QSCALE,
                                                           qst[rows, s, 0, e, :].bitcast(F32),
                                                           ALU.mult, ALU.subtract)
                    ins.then_inc(kq_done, 1)

            def normalise(b, p):
                dve.wait_ge(pv_done, b * PAIRS + (p + 1))
                n = b * PAIRS + p
                dve.reciprocal(on32[:, :], heads_out[:, L:2 * L]).then_inc(rden_done, 1)
                dve.wait_ge(rden_done, n + 1)
                dve.tensor_tensor(on32[:, :], heads_out[:, 0:L], on32[:, :], ALU.mult).then_inc(on_done, 1)
                dve.wait_ge(on_done, n + 1)
                dve.wait_ge(wo_mm, b * 2)
                dve.tensor_copy(oT[:, 0, p, :], on32[:, :]).then_inc(ohi_done, 1)
                dve.wait_ge(ohi_done, n + 1)
                dve.tensor_tensor(oT[:, 1, p, :], on32[:, :], oT[:, 0, p, :].bitcast(F32),
                                  ALU.subtract).then_inc(o_done, 1)

            def statistics(b, go):
                ts = range(4 * go, 4 * go + 4)
                for t in ts:
                    dve.wait_ge(x_in[t], b * 16 + 16)
                    dve.bn_stats(bn[0:ROWS[t], t, :], xin[0:ROWS[t], t, :]).then_inc(bn_done, 1)
                dve.wait_ge(bn_done, b * TILES + (ts[-1] + 1))
                dve.tensor_copy(tick[:, 0:1], halfneg[:, 0:1])
                for t in ts:
                    dve.bn_aggr(mv[0:ROWS[t], t, :], bn[0:ROWS[t], t, :]).then_inc(mv_done, 1)
                dve.wait_ge(mv_done, b * TILES + (ts[-1] + 1))
                if go == 0:
                    dve.tensor_scalar(ve[:, 0:4], mv[:, 0:4, 1], EPS, None, ALU.add).then_inc(ve_done, 1)
                else:
                    dve.tensor_scalar(ve[:, 4:6], mv[:, 4:6, 1], EPS, None, ALU.add).then_inc(ve_done, 1)
                    dve.tensor_scalar(ve[:, 6:8], mv[:, 6:8, 1], 1.0 + EPS, EPS * EPS,
                                      ALU.mult, ALU.add).then_inc(ve_done, 1)

            def centre(b, *ts):
                v = 0 if ts[0] < CTX_TILES else 2
                for t in ts:
                    r = ROWS[t]
                    dve.wait_ge(mv_done, b * TILES + (t + 1))
                    dve.scalar_tensor_tensor(xin[0:r, t, :], xin[0:r, t, :], mv[0:r, t, 0:1],
                                             affine[0:r, v, :], ALU.subtract, ALU.mult).then_inc(gain_done, 1)

            def lo_tile(b, t):
                dve.wait_ge(xhi_done, b * TILES + (t + 1))
                cols = slice(AT[t], AT[t] + ROWS[t])
                dve.tensor_tensor(xT[:, 1, :, cols],
                                  tile_bank(t)[:, :].rearrange("p (k r) -> p k r", k=DC)[:, :, 0:ROWS[t]],
                                  xT[:, 0, :, cols].bitcast(F32), ALU.subtract).then_inc(xlo_done, 1)

            def gated_residual(b):
                for i in range(2):
                    dve.wait_ge(wo_mm, b * 2 + (i + 1))
                    dve.wait_ge(res_in[i], b * 16 + 16)
                    dve.scalar_tensor_tensor(xres[0:LT, i, :], out_bank(i)[0:LT, :], gate[0:LT, 0:1],
                                             xres[0:LT, i, :], ALU.mult, ALU.add).then_inc(x1_done, 1)

            def group_statistics(g, last):
                tiles = tiles_of(last)
                dve.wait_ge(zt_in, g * 16 + 16)
                for i in range(tiles):
                    dve.bn_stats(bn[:, i, :], zt[:, i, :]).then_inc(g_bn, 1)
                dve.wait_ge(g_bn, g * 4 + tiles)
                dve.tensor_copy(tick[:, 0:1], halfneg[:, 0:1])
                for i in range(tiles):
                    dve.bn_aggr(mv[:, i, :], bn[:, i, :]).then_inc(g_mv, 1)
                dve.wait_ge(g_mv, g * 4 + tiles)
                dve.tensor_scalar(ve[:, 0:4], mv[:, 0:4, 1], EPS, None, ALU.add).then_inc(g_ve, 1)

            def group_centre(g, last):
                dve.wait_ge(g_rstd, g + 1)
                for i in range(tiles_of(last)):
                    dve.tensor_scalar(zt[:, i, :], zt[:, i, :], mv[:, i, 0:1], rstd[:, i:i + 1],
                                      ALU.subtract, ALU.mult).then_inc(z_done, 1)

            def group_lo(g, *tiles):
                for i in tiles:
                    dve.wait_ge(z_hi, g * 4 + (i + 1))
                    dve.tensor_tensor(zT[:, 1, :, i * P:(i + 1) * P],
                                      z_bank(g, i)[:, :].rearrange("p (k r) -> p k r", k=DC),
                                      zT[:, 0, :, i * P:(i + 1) * P].bitcast(F32),
                                      ALU.subtract).then_inc(z_lo, 1)

            def split_weights(*pieces):
                for n in pieces:
                    dve.wait_ge(fw_hi, n + 1)
                    dve.tensor_tensor(piece(n, 1), stage(n), piece(n, 0).bitcast(F32),
                                      ALU.subtract).then_inc(fw_lo, 1)

            def denominators(b, h):
                n = b * 4 + (h - 5)
                total = dsum[:, h % 4, :]
                tile = lambda t: probs[0:LT, h % 4, t * L:(t + 1) * L]
                dve.wait_ge(exp_done, b * HEADS + (h + 1))
                dve.tensor_reduce(total[0:CT, :], probs[0:CT, h % 4, 0:CTX_TILES * L].rearrange(
                    "p (t l) -> p l t", t=CTX_TILES), AX.X, ALU.add).then_inc(dve_dchain, 1)
                dve.wait_ge(dve_dchain, n + 1)
                dve.tensor_tensor(total[0:LT, :], total[0:LT, :], tile(CTX_TILES), ALU.add).then_inc(dve_dchain, 1)
                dve.wait_ge(dve_dchain, n + 2)
                dve.tensor_tensor(total[0:LT, :], total[0:LT, :], tile(CTX_TILES + 1),
                                  ALU.add).then_inc(dve_dsum_done, 1)

            def batch(b, last):
                def ahead(*ts):
                    for t in ts:
                        if not last:
                            lo_tile(b + 1, t)
                        elif t < 4:
                            group_lo(0, t)

                subtract(b, 0)
                kq_lo_parts(b, 1, (1, 2))
                scale_max(b, 1)
                subtract(b, 1)
                if not last:
                    statistics(b + 1, 0)
                    centre(b + 1, 0, 1)
                scale_max(b, 2)
                scale_max(b, 3)
                if not last:
                    centre(b + 1, 2, 3)
                subtract(b, 2)
                subtract(b, 3)
                if not last:
                    statistics(b + 1, 1)
                    kq_lo_parts(b, 2)
                    centre(b + 1, 4, 5)
                    centre(b + 1, 6, 7)
                else:
                    group_statistics(0, False)
                    kq_lo_parts(b, 2)
                normalise(b, 0)
                if last:
                    group_centre(0, False)
                scale_max(b, 4)
                scale_max(b, 5)
                kq_lo_parts(b, 3, (0,))
                subtract(b, 4)
                kq_lo_parts(b, 3, (1, 2))
                subtract(b, 5)
                ahead(0)
                normalise(b, 1)
                ahead(1, 2)
                if last:
                    split_weights(0)
                    ahead(3)
                    scale_max(b, 6)
                else:
                    scale_max(b, 6)
                    ahead(3)
                if not last:
                    ahead(4, 5)
                    denominators(b, 5)
                    ahead(6, 7)
                    scale_max(b, 7)
                else:
                    scale_max(b, 7)
                    denominators(b, 5)
                if not last:
                    normalise(b, 2)
                    kq_lo_parts(b + 1, 0)
                    subtract(b, 6)
                    subtract(b, 7)
                else:
                    subtract(b, 6)
                    subtract(b, 7)
                    normalise(b, 2)
                    split_weights(*range(1, 4))
                denominators(b, 7)
                if not last:
                    scale_max(b + 1, 0)
                else:
                    split_weights(*range(4, EARLY))
                normalise(b, 3)
                if not last:
                    kq_lo_parts(b + 1, 1, (0,))
                gated_residual(b)

            def first_offset(*ts):
                for t in ts:
                    r, v = ROWS[t], 1 if t < CTX_TILES else 3
                    dve.wait_ge(scaled, t + 1)
                    dve.tensor_tensor(xin[0:r, t, :], xin[0:r, t, :], affine[0:r, v, :],
                                      ALU.add).then_inc(ln_first, 1)

            def split_lo(i, w):
                dve.wait_ge(w_hi, i + 1)
                dve.tensor_tensor(w[:, 1], staged[i], w[:, 0].bitcast(F32), ALU.subtract).then_inc(w_lo[i], 1)

            dve.memset(ones[:, :], 1.0).then_inc(const_ready, 1)
            dve.memset(halfneg[:, :], -0.5).then_inc(const_ready, 1)
            dve.memset(mv[:, :, :], 1.0).then_inc(const_ready, 1)
            dve.memset(mx[:, :, :], LOWEST).then_inc(pad_ready, 1)
            dve.memset(probs[64:P, :, CTX_TILES * L:], LOWEST).then_inc(pad_ready, 1)
            dve.wait_ge(const_ready, 3)
            statistics(0, 0)
            dve.wait_ge(affine_in[0], 32)
            centre(0, 0, 1, 2, 3)
            statistics(0, 1)
            centre(0, 4, 5)
            dve.wait_ge(affine_in[1], 32)
            centre(0, 6, 7)
            lo_tile(0, 0)
            first_offset(4, 5)
            lo_tile(0, 1)
            lo_tile(0, 2)
            first_offset(6, 7)
            for t in range(3, TILES):
                lo_tile(0, t)
            split_lo(1, wq)
            kq_lo_parts(0, 0)
            split_lo(2, wv)
            scale_max(0, 0)
            split_lo(3, wo)
            dve.wait_ge(gate_half, 1)
            dve.tensor_scalar(gate[:, 1:2], gate[:, 1:2], 1.0 / STEPS, None, ALU.mult).then_inc(gate_ready, 1)
            kq_lo_parts(0, 1, (0,))
            dve.wait_ge(gate_ready, 1)
            with dve.Fori(0, NA - 1) as b:
                batch(b, False)
            batch(NA - 1, True)

            def neuron_op(g, n, last):
                if last:
                    k, half = n // 2, n % 2
                    cur_at, before = 2 + 2 * half, max(n - 1, 0)
                else:
                    half, k = n // 13, n % 13
                    cur_at, before = 2, n - half
                width = DC * (LAST_TG if last else TG) // 2
                y, cur, nxt = (neuron[:, i * width:(i + 1) * width] for i in (half, cur_at, cur_at + 1))
                s = spikes_of(last, half)
                if n == 0 and not last:
                    dve.wait_ge(spkT_mm, g * 4)
                if k == 0:
                    dve.wait_ge(y_done, g * DC + (DC // 2 if half == 0 else DC))
                dve.wait_ge(lif, g * LIF_OPS + before)
                if n == 13 and not last:
                    dve.wait_ge(spk_done, g * 2 + 1)
                if k == 0:
                    ins = dve.tensor_scalar(s, y, THRESHOLD, None, ALU.is_gt)
                elif k == 1:
                    ins = dve.scalar_tensor_tensor(nxt, y, BETA, y, ALU.mult, ALU.add)
                elif k == 2:
                    ins = dve.scalar_tensor_tensor(cur, y, THRESHOLD, nxt, ALU.is_gt, ALU.subtract)
                elif k % 3 == 0:
                    ins = dve.scalar_tensor_tensor(s, cur, -THRESHOLD, s, ALU.is_lt, ALU.add)
                elif k % 3 == 1:
                    ins = dve.scalar_tensor_tensor(nxt, cur, -BETA, y, ALU.mult, ALU.add)
                else:
                    ins = dve.scalar_tensor_tensor(cur, cur, -THRESHOLD, nxt, ALU.is_lt, ALU.subtract)
                ins.then_inc(spk_done if k == 12 else lif, 1)

            def finish(g, tiles, last):
                if last:
                    dve.wait_ge(last_fin_in, 16)
                else:
                    dve.wait_ge(fin_in, g * 16 + 16)
                for i in tiles:
                    dve.wait_ge(spkT_mm, g * 4 + (i + 1))
                    bank = (work[2], heads_out)[i % 2][:, 0:D // 2].bitcast(BF16)
                    rows = fin_of(last)[:, i, :]
                    dve.scalar_tensor_tensor(rows, bank, gate[:, 1:2], rows, ALU.mult,
                                             ALU.add).then_inc(last_fin_done if last else fin_done, 1)

            def h_lo_part(g, j, last):
                n_tok = LAST_TG if last else TG
                dve.wait_ge(h_hi, g * FC + (j + 1))
                dve.tensor_tensor(hT[:, j % 3, 1, 0:n_tok], h32[:, j % 2, 0:n_tok],
                                  hT[:, j % 3, 0, 0:n_tok].bitcast(F32), ALU.subtract).then_inc(h_lo, 1)

            def group(g, first, next_last):
                for j in range(FC):
                    h_lo_part(g, j, False)
                    if first:
                        split_weights(*WITH[j])
                    elif j < 12:
                        for n in range(26 * j // 12, 26 * (j + 1) // 12):
                            neuron_op(g - 1, n, False)
                    elif j in (13, 14):
                        finish(g - 1, (0, 1) if j == 13 else (2, 3), False)
                    if j == 12:
                        group_statistics(g + 1, next_last)
                    if j == 13:
                        group_centre(g + 1, next_last)
                group_lo(g + 1, *range(tiles_of(next_last)))

            def last_group(g):
                for j in range(FC):
                    h_lo_part(g, j, True)
                    if j < FC - 1:
                        for n in range(26 * j // (FC - 1), 26 * (j + 1) // (FC - 1)):
                            neuron_op(g - 1, n, False)
                for n in range(26):
                    neuron_op(g, n, True)
                finish(g, range(LAST_TG // P), True)

            group(0, True, False)
            with dve.Fori(1, GROUPS - 2) as g:
                group(g, False, False)
            group(GROUPS - 2, False, True)
            last_group(GROUPS - 1)

        @block.gpsimd
        def _(pool):
            def all_max(b, h, first=False):
                pool.wait_ge(max_done, b * HEADS + (h + 1))
                if h > 0 or not first:
                    pool.wait_ge(sub_done, b * HEADS + (h - 1))
                    pool.wait_ge(sub_latents, b * HEADS + (h - 1))
                pool.tensor_tensor(tick[:, 1 + h % 2:2 + h % 2], halfneg[:, 0:1], halfneg[:, 0:1], ALU.mult)
                pool.partition_all_reduce(mxb[:, h % 2, :], mx[:, h % 2, :], P, RMAX).then_inc(maxb_done, 1)

            def subtract_latents(b, h):
                v = probs[0:LT, h % 4, CTX_TILES * L:].rearrange("p (t l) -> p t l", t=2)
                pool.wait_ge(maxb_done, b * HEADS + (h + 1))
                pool.tensor_tensor(v, v, mxb[0:LT, h % 2:h % 2 + 1, :].to_broadcast([LT, 2, L]),
                                   ALU.subtract).then_inc(sub_latents, 1)

            def denominators(b, h):
                total = dsum[:, h % 4, :]
                tile = lambda t: probs[0:ROWS[t], h % 4, t * L:(t + 1) * L]
                n = (b * (HEADS - 2) + min(h, 5)) * (TILES - 2)
                pool.wait_ge(exp_done, b * HEADS + (h + 1))
                pool.tensor_tensor(total[0:CT, :], tile(0), tile(1), ALU.add).then_inc(dchain, 1)
                for t in range(2, TILES):
                    pool.wait_ge(dchain, n + (t - 1))
                    pool.tensor_tensor(total[0:ROWS[t], :], total[0:ROWS[t], :], tile(t),
                                       ALU.add).then_inc(dchain if t < TILES - 1 else dsum_done, 1)

            def inverse_root(ready, n, done, lo, hi):
                pool.wait_ge(ready, n)
                pool.tensor_tensor(rstd[:, lo:hi], ve[:, lo:hi], halfneg[:, lo:hi], ALU.pow).then_inc(done, 1)

            def layer_norm_root(b, go):
                inverse_root(ve_done, b * 3 + (1 if go == 0 else 3), rstd_done, 4 * go, 4 * go + 4)

            def offset(b, *ts):
                for t in ts:
                    r, v = ROWS[t], 1 if t < CTX_TILES else 3
                    pool.wait_ge(scaled, b * TILES + (t + 1))
                    pool.tensor_tensor(xin[0:r, t, :], xin[0:r, t, :], affine[0:r, v, :],
                                       ALU.add).then_inc(ln_done, 1)

            def batch(b, last):
                all_max(b, 1)
                subtract_latents(b, 1)
                denominators(b, 0)
                denominators(b, 1)
                if not last:
                    layer_norm_root(b + 1, 0)
                all_max(b, 2)
                all_max(b, 3)
                subtract_latents(b, 2)
                subtract_latents(b, 3)
                if not last:
                    offset(b + 1, 0, 1, 2, 3)
                    layer_norm_root(b + 1, 1)
                else:
                    inverse_root(g_ve, 1, g_rstd, 0, 4)
                denominators(b, 2)
                denominators(b, 3)
                all_max(b, 4)
                all_max(b, 5)
                subtract_latents(b, 4)
                subtract_latents(b, 5)
                if not last:
                    offset(b + 1, 4, 5, 6, 7)
                denominators(b, 4)
                all_max(b, 6)
                subtract_latents(b, 6)
                all_max(b, 7)
                subtract_latents(b, 7)
                denominators(b, 6)
                if not last:
                    all_max(b + 1, 0)
                    subtract_latents(b + 1, 0)

            pool.memset(ident[:, :], 0.0).then_inc(ident_ready, 1)
            pool.memset(ident_b[:, :], 0.0).then_inc(ident_ready, 1)
            pool.wait_ge(ident_ready, 2)
            for m in (ident, ident_b):
                pool.affine_select(out=m[:, :], in_=m[:, :], compare_op=ALU.not_equal, fill=1.0, base=0,
                                   pattern=[[-1, P]], channel_multiplier=1).then_inc(ident_ready, 1)
            pool.wait_ge(const_ready, 3)
            layer_norm_root(0, 0)
            pool.wait_ge(affine_in[0], 32)
            offset(0, 0, 1)
            layer_norm_root(0, 1)
            offset(0, 2, 3)
            pool.wait_ge(w_hi, 1)
            pool.tensor_tensor(wk[:, 1], staged[0], wk[:, 0].bitcast(F32), ALU.subtract).then_inc(w_lo[0], 1)
            all_max(0, 0, True)
            subtract_latents(0, 0)
            with pool.Fori(0, NA - 1) as b:
                batch(b, False)
            batch(NA - 1, True)

            def squares(g, j, last):
                n_tok = LAST_TG if last else TG
                pool.wait_ge(relu_done, g * FC + (j + 1))
                pool.wait_ge(h_lo, g * FC + max(j - 1, 0))
                pool.tensor_tensor(h32[:, j % 2, 0:n_tok], relu[:, j % 2, 0:n_tok], relu[:, j % 2, 0:n_tok],
                                   ALU.mult).then_inc(h_done, 1)

            def group(g, last):
                for j in range(FC):
                    squares(g, j, last)
                    if not last and j == FC - 3:
                        inverse_root(g_ve, g + 2, g_rstd, 0, 4)

            pool.wait_ge(o_done, NA * PAIRS)
            with pool.Fori(0, GROUPS - 1) as g:
                group(g, False)
            group(GROUPS - 1, True)
            for i in range(4):
                if i == 0:
                    pool.wait_ge(fin_in, (GROUPS - 2) * 16 + 16)
                pool.wait_ge(fin_scaled, i + 1)
                pool.tensor_tensor(fin[:, i, :], zt[:, i % 2, :], fin[:, i, :], ALU.add).then_inc(fin_done, 1)


_ORDER = ["x", "ctx_1024", "g_xattn", "g_ffn", "L0_xattn_Wq", "L0_xattn_Wkv", "L0_xattn_Wout", "L0_xattn_gm",
          "L0_xattn_bm", "L0_xattn_gl", "L0_xattn_bl", "L0_ffn_W_fc", "L0_ffn_W_proj"]


def kernel(**inputs):
    import numpy as np
    import concourse.bacc as bacc
    from concourse import mybir as mb
    from concourse.bass_utils import run_bass_kernel_spmd

    def laid_out(name):
        a = np.asarray(inputs[name])
        if name in ("g_xattn", "g_ffn"):
            a = np.repeat(a.reshape(1, 1), 128, axis=0)
        elif name.startswith("L0_ffn"):
            a = a.T
        return np.ascontiguousarray(a)

    nc = bacc.Bacc("TRN2", target_bir_lowering=False, num_devices=1)
    arrays, args = {}, []
    for name in _ORDER:
        a = laid_out(name)
        arrays[f"in_{name}"] = a
        args.append(nc.dram_tensor(f"in_{name}", a.shape, mb.dt.from_np(a.dtype), kind="ExternalInput").ap())
    shape = np.asarray(inputs["x"]).shape
    args.append(nc.dram_tensor("out", shape, mb.dt.float32, kind="ExternalOutput").ap())
    flamingo_block(nc, *args)
    r = run_bass_kernel_spmd(nc, [arrays], core_ids=[0])
    return r.results[0]["out"]
```
